# Optimizing a Trainium2 kernel written in Bass

```python
import numpy as np
import jax
import jax.numpy as jnp

def _softmax(x, axis=-1):
    return jax.nn.softmax(x, axis=axis)

def _gelu(x):
    return jax.nn.gelu(x, approximate=True)

def _silu(x):
    return jax.nn.silu(x)

def _sigmoid(x):
    return jax.nn.sigmoid(x)

def _layernorm(x, axis=-1, eps=1e-05):
    m = jnp.mean(x, axis=axis, keepdims=True)
    v = jnp.var(x, axis=axis, keepdims=True)
    return (x - m) / jnp.sqrt(v + eps)

def _scatter_add(tgt, idx, src, axis=0):
    return tgt.at[idx].add(src)

def _segment_sum(src, seg, n):
    return jax.ops.segment_sum(src, seg, n)
kernel_name = 'mk_xattn_ffn_d1_seqx_r4_524858'

def setup_inputs(seed: int=0):
    np.random.seed(seed)
    _w = jnp.asarray

    def _rec_inputs():
        import jax
        import jax.numpy as jnp
        _rk = jax.random.key(seed)
        x = -0.000125 + 0.9999 * jax.random.normal(jax.random.fold_in(_rk, 1), (2, 1024, 256), jnp.float32)
        _lenS = 1024 - jax.random.randint(jax.random.fold_in(_rk, 7), (2,), 0, max(1, 1024 // 4) + 1, jnp.int32)
        _lenS2 = 77 - jax.random.randint(jax.random.fold_in(_rk, 8), (2,), 0, max(1, 77 // 4) + 1, jnp.int32)
        _ctx_768P = jax.random.normal(jax.random.fold_in(_rk, 11), (2, 16, 192), jnp.float32)
        _ctx_768c = jax.random.dirichlet(jax.random.fold_in(_rk, 511), 0.3 * jnp.ones((16,), jnp.float32), (2, 77))
        _ctx_768t = jnp.einsum('bsk,bkd->bsd', _ctx_768c, _ctx_768P)
        _ctx_768t = _ctx_768t * jax.lax.rsqrt(jnp.mean(jnp.square(_ctx_768t)) + 1e-12) * 0.953939
        ctx_768 = -0.000191848 + 0.999787 * (_ctx_768t + 0.3 * jax.random.normal(jax.random.fold_in(_rk, 611), (2, 77, 192), jnp.float32))
        return (x, ctx_768)
    x, ctx_768 = _rec_inputs()

    def _L0_xattn_setup():
        import jax, jax.numpy as jnp
        import numpy as np
        NUM_HEADS = 8
        DIM_HEAD = 128
        SCALE = DIM_HEAD ** (-0.25)
        key = jax.random.key(seed)
        ks = jax.random.split(key, 7)
        B, Tq, Dq = (8, 1024, 256)
        Tk, Dc = (256, 192)
        inner = NUM_HEADS * DIM_HEAD
        s = lambda d: 1.0 / np.sqrt(d)
        return {'x': jax.random.normal(ks[0], (B, Tq, Dq), jnp.float32), 'context': jax.random.normal(ks[1], (B, Tk, Dc), jnp.float32), 'Wq': jax.random.normal(ks[2], (Dq, inner), jnp.float32) * s(Dq), 'Wk': jax.random.normal(ks[3], (Dc, inner), jnp.float32) * s(Dc), 'Wv': jax.random.normal(ks[4], (Dc, inner), jnp.float32) * s(Dc), 'Wo': jax.random.normal(ks[5], (inner, Dq), jnp.float32) * s(inner), 'bo': jnp.zeros((Dq,), jnp.float32)}
    _L0_xattn_all = _L0_xattn_setup()
    _L0_xattn_in = {k: v for k, v in _L0_xattn_all.items() if k in ('Wq', 'Wk', 'Wv', 'Wo', 'bo')}
    del _L0_xattn_all

    def _L0_ffn_setup():
        import jax, jax.numpy as jnp
        import numpy as np
        D_MODEL = 256
        EXPERT_DIM = 128
        N_EXPERTS = 8
        TOP_K = 2

        def _sq_relu(h):
            return jnp.square(jax.nn.relu(h))
        key = jax.random.key(seed)
        ks = jax.random.split(key, 6)
        s = 0.02
        x = jax.random.normal(ks[0], (2, 512, D_MODEL), dtype=jnp.float32)
        Ws1 = jax.random.normal(ks[1], (D_MODEL, EXPERT_DIM), dtype=jnp.float32) * s
        Ws2 = jax.random.normal(ks[2], (EXPERT_DIM, D_MODEL), dtype=jnp.float32) * s
        W1 = jax.random.normal(ks[3], (N_EXPERTS, D_MODEL, EXPERT_DIM), dtype=jnp.float32) * s
        W2 = jax.random.normal(ks[4], (N_EXPERTS, EXPERT_DIM, D_MODEL), dtype=jnp.float32) * s
        Wr = jax.random.normal(ks[5], (D_MODEL, N_EXPERTS), dtype=jnp.float32) * s
        return {'x': x, 'Ws1': Ws1, 'Ws2': Ws2, 'W1': W1, 'W2': W2, 'Wr': Wr}
    _L0_ffn_all = _L0_ffn_setup()
    _L0_ffn_in = {k: v for k, v in _L0_ffn_all.items() if k in ('Ws1', 'Ws2', 'W1', 'W2', 'Wr')}
    del _L0_ffn_all
    return {'x': x, 'ctx_768': ctx_768, 'L0_xattn_Wq': _L0_xattn_in['Wq'], 'L0_xattn_Wk': _L0_xattn_in['Wk'], 'L0_xattn_Wv': _L0_xattn_in['Wv'], 'L0_xattn_Wo': _L0_xattn_in['Wo'], 'L0_xattn_bo': _L0_xattn_in['bo'], 'L0_ffn_Ws1': _L0_ffn_in['Ws1'], 'L0_ffn_Ws2': _L0_ffn_in['Ws2'], 'L0_ffn_W1': _L0_ffn_in['W1'], 'L0_ffn_W2': _L0_ffn_in['W2'], 'L0_ffn_Wr': _L0_ffn_in['Wr']}

def reference(x, ctx_768, L0_xattn_Wq, L0_xattn_Wk, L0_xattn_Wv, L0_xattn_Wo, L0_xattn_bo, L0_ffn_Ws1, L0_ffn_Ws2, L0_ffn_W1, L0_ffn_W2, L0_ffn_Wr):
    import jax
    import jax.numpy as jnp

    def _L0_xattn_ref(x, context, Wq, Wk, Wv, Wo, bo):
        import jax, jax.numpy as jnp
        import numpy as np
        NUM_HEADS = 8
        DIM_HEAD = 128
        SCALE = DIM_HEAD ** (-0.25)
        B, Tq, _ = x.shape
        Tk = context.shape[1]
        h, C = (NUM_HEADS, DIM_HEAD)
        q = (x @ Wq).reshape(B, Tq, h, C) * SCALE
        k = (context @ Wk).reshape(B, Tk, h, C) * SCALE
        v = (context @ Wv).reshape(B, Tk, h, C)
        attn = jax.nn.softmax(jnp.einsum('bqhc,bkhc->bhqk', q, k), axis=-1)
        out = jnp.einsum('bhqk,bkhc->bqhc', attn, v).reshape(B, Tq, h * C)
        return out @ Wo + bo

    def _L0_ffn_ref(x, Ws1, Ws2, W1, W2, Wr):
        import jax, jax.numpy as jnp
        import numpy as np
        D_MODEL = 256
        EXPERT_DIM = 128
        N_EXPERTS = 8
        TOP_K = 2

        def _sq_relu(h):
            return jnp.square(jax.nn.relu(h))
        shape = x.shape
        xf = x.reshape(-1, D_MODEL)
        out_shared = _sq_relu(xf @ Ws1) @ Ws2
        logits = xf @ Wr
        top_vals, top_idx = jax.lax.top_k(logits, TOP_K)
        rw = jax.nn.softmax(top_vals.astype(jnp.float32), axis=-1).astype(x.dtype)
        onehot = jax.nn.one_hot(top_idx, N_EXPERTS, dtype=x.dtype)
        prob = jnp.einsum('tk,tke->te', rw, onehot)
        prob = jnp.trunc(prob)
        h = _sq_relu(jnp.einsum('td,edf->tef', xf, W1))
        y = jnp.einsum('tef,efd->ted', h, W2)
        out_routed = jnp.einsum('ted,te->td', y, prob)
        return (out_shared + out_routed).reshape(shape)
    x = x + _L0_xattn_ref(_layernorm(x, axis=-1), ctx_768, L0_xattn_Wq, L0_xattn_Wk, L0_xattn_Wv, L0_xattn_Wo, L0_xattn_bo)
    x = x + _L0_ffn_ref(_layernorm(x, axis=-1), L0_ffn_Ws1, L0_ffn_Ws2, L0_ffn_W1, L0_ffn_W2, L0_ffn_Wr)
    return x

_drawn_inputs = setup_inputs


def setup_inputs(seed=0):
    import zlib

    import numpy as np

    out = dict(_drawn_inputs(seed))
    spreads = {'L0_xattn_bo': (0.0, 0.1)}
    factors = {}
    for name, (base, spread) in spreads.items():
        noise = np.random.default_rng([zlib.crc32(name.encode()), seed]).standard_normal(out[name].shape)
        drawn = base * np.exp(spread * noise) if base else spread * noise
        out[name] = jnp.asarray(drawn.astype(out[name].dtype))
    for name, factor in factors.items():
        out[name] = (out[name] * factor).astype(out[name].dtype)
    return out
```

```python
from contextlib import ExitStack

import concourse.bass as bass
from concourse import mybir
from concourse.alu_op_type import AluOpType as ALU

F32 = mybir.dt.float32
F32R = mybir.dt.float32r
I32 = mybir.dt.int32
ACT = mybir.ActivationFunctionType
X = mybir.AxisListType.X

P = 128
EPS = 1e-5


def live(t, tiles):
    return not isinstance(t, int) or 0 <= t < tiles


def program(nc, x, x_t, ctx_t, wq_t, wk, wv, wo, bo, ws1, ws2, w1, w2, wr, out):
    B, TQ, D = x.shape
    TK = ctx_t.shape[1] // B
    DC = ctx_t.shape[0]
    H = wk.shape[1] // P
    E, _, FE = w1.shape
    DCH = D // P
    CP = DC // 2
    BK = B * TK
    HK = H * TK
    HALF = H // 2 * TK
    KC = -(-HK // P)
    KLAST = HK - (KC - 1) * P
    TILES = B * TQ // P
    NL = FE + E
    SCALE2 = float(P) ** -0.5
    assert B == 2 and FE == P and TILES % 4 == 0 and HALF <= 512 and KC == 5 and DCH == 2
    WFFN_STEPS = 5
    GATE_STEPS = 8
    XO = KC * P
    HO = XO + D

    u_rows = nc.dram_tensor("u_rows", (B, HK, D), F32, kind="Internal").ap()

    with ExitStack() as ctx:
        def sb(name, shape, dt=F32):
            return ctx.enter_context(nc.sbuf_tensor(name, shape, dt))

        def psum(name, shape):
            return ctx.enter_context(nc.psum_tensor(name, shape, F32))

        def sem(name):
            return ctx.enter_context(nc.semaphore(name))

        ctx_sb = sb("ctx_sb", [CP, 2, BK])
        wk_sb = sb("wk_sb", [CP, 2, H * P])
        wv_sb = sb("wv_sb", [CP, 2, H * P])
        wqt_sb = sb("wqt_sb", [P, H, D])
        wq_mean = sb("wq_mean", [P, 2, H])
        wo_sb = sb("wo_sb", [P, H, D])
        kt_sb = sb("kt_sb", [P, H, BK])
        vt_sb = sb("vt_sb", [P, H, BK])
        a_hi = sb("a_hi", [P, DCH, B, HK], F32R)
        a_lo = sb("a_lo", [P, DCH, B, HK], F32R)
        u_stage = sb("u_stage", [TK, B, H, D])
        u_sb = sb("u_sb", [P, B, KC, D])
        u_hi = sb("u_hi", [P, B, KC, D], F32R)
        u_lo = sb("u_lo", [P, B, KC, D], F32R)
        bo_sb = sb("bo_sb", [P, D])
        wsr_sb = sb("wsr_sb", [P, DCH, NL])
        wsr_c = sb("wsr_c", [P, DCH, NL])
        wsr_hi = sb("wsr_hi", [P, DCH, NL], F32R)
        wsr_lo = sb("wsr_lo", [P, DCH, NL], F32R)
        ws2_sb = sb("ws2_sb", [P, D])
        ws2_hi = sb("ws2_hi", [P, D], F32R)
        ws2_lo = sb("ws2_lo", [P, D], F32R)
        ident = sb("ident", [P, P])
        mean_of = sb("mean_of", [P, P])
        pow_neg = sb("pow_neg", [P, 1])
        pow_pos = sb("pow_pos", [P, TILES])
        x_sb = sb("x_sb", [P, TILES, D])
        xt_sb = sb("xt_sb", [P, DCH, B, TQ])
        xb_sb = sb("xb_sb", [P, 2, D])
        x1_sb = sb("x1_sb", [P, TILES, D])
        y_sb = sb("y_sb", [P, TILES, D])
        xt_hi = sb("xt_hi", [P, 2, DCH, P], F32R)
        xt_lo = sb("xt_lo", [P, 2, DCH, P], F32R)
        probs = sb("probs", [P, 2, KC * P])
        g_hi = sb("g_hi", [P, HO + P], F32R)
        g_lo = sb("g_lo", [P, HO + P], F32R)
        x1_tr = sb("x1_tr", [P, 2, D])
        h_relu = sb("h_relu", [P, 2, FE])
        h2 = sb("h2", [P, 2, FE])
        bn1 = sb("bn1", [P, 2, 6])
        bn2 = sb("bn2", [P, 2, 6])
        mv1 = sb("mv1", [P, 2, 2])
        mv2 = sb("mv2", [P, 2, 2])
        var1 = sb("var1", [P, 2])
        rstd1 = sb("rstd1", [P, 2])
        var2 = sb("var2", [P, 2])
        row_max = sb("row_max", [P, 2, H])
        neg_max = sb("neg_max", [P, 2, H])
        sums = sb("sums", [P, 2, H])
        recip = sb("recip", [P, 2, H])
        top8 = sb("top8", [P, 2, 8])
        rvar2 = sb("rvar2", [P, TILES])
        rstd2 = sb("rstd2", [P, TILES])
        logits = sb("logits", [P, TILES, E])
        gap = sb("gap", [P, TILES])
        gap_s = sb("gap_s", [P, TILES])
        gap_e = sb("gap_e", [P, TILES])
        gap_d = sb("gap_d", [P, TILES])
        gate = sb("gate", [P, TILES])
        gate_any = sb("gate_any", [P, 1])
        flag = sb("flag", [1, 1], I32)
        assert E == H and DCH * FE == D
        w1_sb = wqt_sb[:, :, :].rearrange("p e (c f) -> p e c f", c=DCH)
        w2_sb = wo_sb
        gate_e = sb("gate_e", [P, E])
        gate_max = sb("gate_max", [P, 1])
        r_bn = sb("r_bn", [P, 6])
        r_mv = sb("r_mv", [P, 2])
        xt_flat = xt_sb[:, 0, :, :].rearrange("p b n -> p (b n)")
        xn = x_sb[:, 0, :]
        xnt = x_sb[:, 1, :].rearrange("p (c n) -> p c n", c=DCH)
        hr = xt_flat[:, 0:E * P].rearrange("p (e n) -> p e n", e=E)

        s_ps = psum("s_ps", [P, 4, 512])
        g_ps = psum("g_ps", [P, 1024])
        o_ps = psum("o_ps", [P, 512])
        f_ps = psum("f_ps", [P, 512])
        routed_banks = [s_ps[:, 2, :], s_ps[:, 3, :], o_ps[:, :], f_ps[:, :]]
        once_banks = [g_ps[:, 0:512], g_ps[:, 512:1024], o_ps[:, :], f_ps[:, :]]

        ctx_in, wk_in, wsr_in, wv_in, wo_in, bo_in = (sem(n) for n in ("ctx_in", "wk_in", "wsr_in", "wv_in", "wo_in", "bo_in"))
        ws2_in = sem("ws2_in")
        wq_in = [sem(f"wq_in{i}") for i in range(2)]
        xt_in = [sem(f"xt_in{i}") for i in range(4)]
        x_in = [sem(f"x_in{i}") for i in range(4)]
        u_out = [sem(f"u_out{b}") for b in range(B)]
        u_in = [sem(f"u_in{b}") for b in range(B)]
        y_out = sem("y_out")
        w12_in = sem("w12_in")
        const_ready = sem("const_ready")
        fill_ready = sem("fill_ready")
        wmean_ready = sem("wmean_ready")
        kt_ready = sem("kt_ready")
        kt_copied = sem("kt_copied")
        vt_ready = sem("vt_ready")
        vt_copied = sem("vt_copied")
        wqs = sem("wqs")
        wq_ready = sem("wq_ready")
        a_ready = sem("a_ready")
        ahi_ready = sem("ahi_ready")
        alo_ready = sem("alo_ready")
        wffn = sem("wffn")
        u_ready = sem("u_ready")
        u_staged = sem("u_staged")
        uhi_ready = sem("uhi_ready")
        ulo_ready = sem("ulo_ready")
        bn1_done, mv1_done, var1_done = sem("bn1_done"), sem("mv1_done"), sem("var1_done")
        rstd1_done = sem("rstd1_done")
        xthi_first, xthi_done, xt_ready = sem("xthi_first"), sem("xthi_done"), sem("xt_ready")
        s_ready = sem("s_ready")
        max_done, negmax_ready = sem("max_done"), sem("negmax_ready")
        exp_done = sem("exp_done")
        recip_ready = sem("recip_ready")
        probs_ready = sem("probs_ready")
        xb_ready = sem("xb_ready")
        g_ready = sem("g_ready")
        ghi_ready, glo_ready = sem("ghi_ready"), sem("glo_ready")
        o_ready = sem("o_ready")
        x1_ready = sem("x1_ready")
        x1_kept = sem("x1_kept")
        bn2_done, mv2_done, var2_done, rvar2_done = (sem(n) for n in ("bn2_done", "mv2_done", "var2_done", "rvar2_done"))
        hl_ready = sem("hl_ready")
        relu_done, h2_ready = sem("relu_done"), sem("h2_ready")
        top_done, logits_done = sem("top_done"), sem("logits_done")
        ffn_ready = sem("ffn_ready")
        y_ready = sem("y_ready")
        gs = sem("gs")
        r_x, r_xt, r_xtc, r_h, r_hc, r_y, r_relu, r_acc, r_out, r_dve = (sem(n) for n in ("r_x", "r_xt", "r_xtc", "r_h", "r_hc", "r_y", "r_relu", "r_acc", "r_out", "r_dve"))

        def second_bank(t):
            if not isinstance(t, int):
                return 512, HO + P
            return (512 if t < TILES else XO if t == TILES else HO), (XO if t == 0 else HO if t == 1 else HO + P)

        x_rows = x.rearrange("b (n p) d -> p n b d", p=P)
        out_rows = out.rearrange("b (n p) d -> p n b d", p=P)
        xt_rows = x_t.rearrange("(c p) (b n) -> p c b n", p=P, b=B)
        y_pairs = y_sb[:, :, :].rearrange("p (n b) d -> p n b d", b=B)
        x_pairs = x_sb[:, :, :].rearrange("p (n b) d -> p n b d", b=B)
        NB = TQ // P
        GB = NB // 4

        def pairs(eng, first, last, step):
            with eng.Fori(first // 2, last // 2) as j:
                for par in range(2):
                    step(2 * j + par, par)

        def wait_apart(eng, semaphore, count):
            eng.wait_ge(const_ready, 4)
            eng.wait_ge(semaphore, count)

        block = ctx.enter_context(nc.Block())

        @block.sync
        def _(sp):
            sp.dma_start(ctx_sb[:, :, :], ctx_t.rearrange("(c p) n -> p c n", p=CP)).then_inc(ctx_in, 16)
            sp.dma_start(wk_sb[:, :, :], wk.rearrange("(c p) n -> p c n", p=CP)).then_inc(wk_in, 16)
            for i in range(2):
                sp.dma_start(wqt_sb[:, i * H // 2:(i + 1) * H // 2, :],
                             wq_t.rearrange("(h p) d -> p h d", p=P)[:, i * H // 2:(i + 1) * H // 2, :]).then_inc(wq_in[i], 16)
            sp.dma_start(wsr_sb[:, :, 0:FE], ws1.rearrange("(c p) f -> p c f", p=P)).then_inc(wsr_in, 16)
            sp.dma_start(wsr_sb[:, :, FE:NL], wr.rearrange("(c p) e -> p c e", p=P)).then_inc(wsr_in, 16)

            def load_x(i):
                for c in range(DCH):
                    sp.dma_start(xt_sb[:, c, :, i * GB * P:(i + 1) * GB * P],
                                 xt_rows[:, c, :, i * GB * P:(i + 1) * GB * P]).then_inc(xt_in[i], 16)
                for b in range(B):
                    sp.dma_start(x_pairs[:, i * GB:(i + 1) * GB, b, :], x_rows[:, i * GB:(i + 1) * GB, b, :]).then_inc(x_in[i], 16)

            load_x(0)
            sp.dma_start(wv_sb[:, :, :], wv.rearrange("(c p) n -> p c n", p=CP)).then_inc(wv_in, 16)
            sp.dma_start(wo_sb[:, :, :], wo.rearrange("(h p) d -> p h d", p=P)).then_inc(wo_in, 16)
            sp.dma_start(ws2_sb[:, :], ws2).then_inc(ws2_in, 16)
            sp.dma_start(bo_sb[:, :], bo.rearrange("(a d) -> a d", a=1).broadcast_to([P, D])).then_inc(bo_in, 16)
            for b in range(B):
                sp.wait_ge(u_staged, 4 * (b + 1))
                sp.dma_start(u_rows[b].rearrange("(h k) d -> k h d", k=TK), u_stage[:, b, :, :]).then_inc(u_out[b], 16)
                sp.wait_ge(u_out[b], 16)
                sp.dma_start(u_sb[:, b, 0:KC - 1, :],
                             u_rows[b, 0:(KC - 1) * P, :].rearrange("(c p) d -> p c d", p=P)).then_inc(u_in[b], 16)
                sp.dma_start(u_sb[0:KLAST, b, KC - 1, :], u_rows[b, (KC - 1) * P:HK, :]).then_inc(u_in[b], 16)
                if b == 0:
                    load_x(1)
            load_x(2)
            load_x(3)

            def keep_x1(k):
                sp.wait_ge(x1_ready, 2 * k + 2)
                sp.dma_start(x1_sb[:, bass.ds(2 * k, 2), :], x1_tr[:, :, :]).then_inc(x1_kept, 16)

            def store(k):
                sp.wait_ge(y_ready, 2 * k + 2)
                sp.dma_start(out_rows[:, k, :, :], y_sb[:, bass.ds(2 * k, 2), :]).then_inc(y_out, 16)

            keep_x1(0)
            with sp.Fori(1, NB) as k:
                keep_x1(k)
                store(k - 1)
            store(NB - 1)
            sp.wait_ge(y_out, 16 * NB)

            sp.wait_ge(gs, GATE_STEPS)
            any_open = sp.value_load(flag[0:1, 0:1], min_val=0, max_val=1)
            with sp.If(any_open > 0):
                sp.dma_start(w1_sb[:, :, :, :].rearrange("p e c f -> p (e c) f"),
                             w1.rearrange("e (c p) f -> p (e c) f", p=P)).then_inc(w12_in, 16)
                sp.dma_start(w2_sb[:, :, :], w2.rearrange("e p d -> p e d")).then_inc(w12_in, 16)
                with sp.Fori(0, NB) as k:
                    sp.wait_ge(r_acc, 2 * k + 2)
                    sp.dma_start(out_rows[:, k, :, :], y_sb[:, bass.ds(2 * k, 2), :]).then_inc(r_out, 16)
                sp.wait_ge(r_out, 16 * NB)

        @block.tensor
        def _(pe):
            def mean_weights():
                pe.wait_ge(wsr_in, 32)
                pe.wait_ge(fill_ready, 1)
                for c in range(DCH):
                    mm = pe.matmul(f_ps[:, 0:NL], mean_of[:, :], wsr_sb[:, c, :], start=c == 0, stop=c == DCH - 1)
                mm.then_inc(wmean_ready, 1)

            def context_rows(w, ready, bank_free):
                for g in range(H // 2):
                    if bank_free is not None:
                        pe.wait_ge(bank_free, g + 1)
                    for h in (2 * g, 2 * g + 1):
                        for c in range(2):
                            mm = pe.matmul(s_ps[:, g, (h % 2) * BK:(h % 2 + 1) * BK], w[:, c, h * P:(h + 1) * P],
                                           ctx_sb[:, c, :], start=c == 0, stop=c == 1)
                    mm.then_inc(ready, 1)

            def make_a():
                for h in range(H):
                    pe.wait_ge(kt_copied, h // 2 + 1)
                    pe.wait_ge(wq_ready, h // (H // 2) + 1)
                    if h == 3:
                        pe.wait_ge(wffn, 1)
                    if h >= 4:
                        pe.wait_ge(alo_ready, h - 3)
                    for c in range(DCH):
                        mm = pe.matmul(once_banks[h % 4][:, c * BK:(c + 1) * BK], wqt_sb[:, h, c * P:(c + 1) * P],
                                       kt_sb[:, h, :], start=True, stop=True)
                    mm.then_inc(a_ready, 1)

            def make_u(b):
                for g in range(H // 2):
                    if b == 0:
                        pe.wait_ge(vt_copied, g + 1)
                        pe.wait_ge(alo_ready, H - 3 + g)
                    else:
                        pe.wait_ge(u_staged, g + 1)
                    for i in range(2):
                        h = 2 * g + i
                        mm = pe.matmul(once_banks[g][0:TK, i * D:(i + 1) * D], vt_sb[:, h, b * TK:(b + 1) * TK],
                                       wo_sb[:, h, :], start=True, stop=True)
                    mm.then_inc(u_ready, 1)

            def three(out_ap, hi, lo, rhs_hi, rhs_lo, first, last):
                pe.matmul(out_ap, hi, rhs_hi, start=first, stop=False)
                pe.matmul(out_ap, lo, rhs_hi, start=False, stop=False)
                return pe.matmul(out_ap, hi, rhs_lo, start=False, stop=last)

            def scores(t, par):
                pe.wait_ge(xt_ready, t + 1)
                if not isinstance(t, int) or t >= 2:
                    pe.wait_ge(exp_done, 2 * t - 2)
                for half in range(2):
                    for c in range(DCH):
                        cols = slice(half * HALF, (half + 1) * HALF)
                        mm = three(s_ps[:, 2 * par + half, 0:HALF], xt_hi[:, par, c, :], xt_lo[:, par, c, :],
                                   a_hi[:, c, par, cols], a_lo[:, c, par, cols], c == 0, c == DCH - 1)
                mm.then_inc(s_ready, 1)

            def step(t, par):
                if not isinstance(t, int) or t >= 1:
                    pe.wait_ge(glo_ready, 2 * t)
                mm = None
                if live(t, TILES):
                    pe.wait_ge(probs_ready, 2 * t + 1)
                    for c in range(KC):
                        if (c + 1) * P > HALF and c * P <= HALF:
                            pe.wait_ge(probs_ready, 2 * t + 2)
                        mm = pe.transpose(g_ps[:, c * P:(c + 1) * P], probs[:, par, c * P:(c + 1) * P], ident[:, :])
                        if (c + 1) * P == 512:
                            mm.then_inc(g_ready, 1)
                if live(t - 1, TILES):
                    pe.wait_ge(x1_ready, t)
                    for c in range(DCH):
                        mm = pe.transpose(g_ps[:, XO + c * P:XO + (c + 1) * P],
                                          x1_tr[:, 1 - par, c * P:(c + 1) * P], ident[:, :])
                if live(t - 2, TILES):
                    pe.wait_ge(h2_ready, t - 1)
                    mm = pe.transpose(g_ps[:, HO:HO + P], h2[:, par, :], ident[:, :])
                mm.then_inc(g_ready, 1 if live(t, TILES) else 2)

                if live(t + 2, TILES):
                    scores(t + 2, par)

                if live(t, TILES):
                    if isinstance(t, int) and t < 2:
                        pe.wait_ge(uhi_ready, t + 1)
                        pe.wait_ge(ulo_ready, t + 1)
                    pe.wait_ge(glo_ready, 2 * t + 1)
                    for c in range(KC):
                        if (c + 1) * P > 512:
                            pe.wait_ge(glo_ready, 2 * t + 2)
                        k = P if c < KC - 1 else KLAST
                        mm = three(o_ps[:, 0:D], g_hi[0:k, c * P:(c + 1) * P], g_lo[0:k, c * P:(c + 1) * P],
                                   u_hi[0:k, par, c, :], u_lo[0:k, par, c, :], c == 0, c == KC - 1)
                    mm.then_inc(o_ready, 1)
                else:
                    pe.wait_ge(glo_ready, 2 * t + 2)

                if live(t - 2, TILES):
                    pe.wait_ge(logits_done, t - 1)
                    if not isinstance(t, int) or t >= 3:
                        pe.wait_ge(y_ready, t - 2)
                    three(f_ps[:, 0:D], g_hi[:, HO:HO + P], g_lo[:, HO:HO + P],
                          ws2_hi[:, :], ws2_lo[:, :], True, True).then_inc(ffn_ready, 1)
                if live(t - 1, TILES):
                    for c in range(DCH):
                        cols = slice(XO + c * P, XO + (c + 1) * P)
                        mm = three(f_ps[:, D:D + NL], g_hi[:, cols], g_lo[:, cols],
                                   wsr_hi[:, c, :], wsr_lo[:, c, :], c == 0, c == DCH - 1)
                    mm.then_inc(hl_ready, 1)

            mean_weights()
            pe.wait_ge(ctx_in, 16)
            pe.wait_ge(wk_in, 16)
            context_rows(wk_sb, kt_ready, None)
            make_a()
            pe.wait_ge(wv_in, 16)
            context_rows(wv_sb, vt_ready, kt_copied)
            pe.wait_ge(wo_in, 16)
            make_u(0)
            pe.wait_ge(vt_copied, H // 2)
            scores(0, 0)
            scores(1, 1)
            make_u(1)
            pe.wait_ge(const_ready, 4)
            pe.wait_ge(u_staged, H)
            pe.wait_ge(wffn, WFFN_STEPS)
            step(0, 0)
            step(1, 1)
            pairs(pe, 2, TILES - 2, step)
            for t in range(TILES - 2, TILES + 2):
                step(t, t % 2)

            pe.wait_ge(gs, GATE_STEPS - 2)
            pe.matmul(o_ps[0:1, 0:1], gate_any[:, 0:1], mean_of[:, 0:1], start=True, stop=True).then_inc(gs, 1)
            pe.wait_ge(gs, GATE_STEPS)
            any_open = pe.value_load(flag[0:1, 0:1], min_val=0, max_val=1)
            with pe.If(any_open > 0):
                pe.wait_ge(w12_in, 32)
                with pe.Fori(0, TILES) as t:
                    pe.wait_ge(r_x, t + 1)
                    for c in range(DCH):
                        mm = pe.transpose(g_ps[:, c * P:(c + 1) * P], xn[:, c * P:(c + 1) * P], ident[:, :])
                    mm.then_inc(r_xt, 1)
                    pe.wait_ge(r_xtc, t + 1)
                    for e in range(E):
                        for c in range(DCH):
                            mm = pe.matmul(s_ps[:, e // 4, (e % 4) * P:(e % 4 + 1) * P], w1_sb[:, e, c, :], xnt[:, c, :],
                                           start=c == 0, stop=c == DCH - 1)
                    mm.then_inc(r_h, 1)
                    pe.wait_ge(r_hc, t + 1)
                    for e in range(E):
                        mm = pe.matmul(routed_banks[e // 2][:, (e % 2) * D:(e % 2 + 1) * D], hr[:, e, :], w2_sb[:, e, :],
                                       start=True, stop=True)
                    mm.then_inc(r_y, 1)

        @block.scalar
        def _(act):
            def hi_of_transposes(t, par):
                if live(t, TILES):
                    act.wait_ge(g_ready, 2 * t + 1)
                    act.activation(g_hi[:, 0:512], g_ps[:, 0:512], ACT.Copy).then_inc(ghi_ready, 1)
                act.wait_ge(g_ready, 2 * t + 2)
                lo, hi = second_bank(t)
                act.activation(g_hi[:, lo:hi], g_ps[:, lo:hi], ACT.Copy).then_inc(ghi_ready, 1 if live(t, TILES) else 2)

            def exps(t, par, half):
                if half == 0:
                    act.wait_ge(negmax_ready, t + 1)
                for h in range(half * H // 2, (half + 1) * H // 2):
                    e = act.activation(probs[:, par, h * TK:(h + 1) * TK],
                                       s_ps[:, 2 * par + half, (h - half * H // 2) * TK:(h - half * H // 2 + 1) * TK],
                                       ACT.Exp, bias=neg_max[:, par, h:h + 1], scale=rstd1[:, par:par + 1],
                                       accum_out=sums[:, par, h:h + 1])
                e.then_inc(exp_done, 1)

            def relu(t, par):
                act.wait_ge(hl_ready, t + 1)
                act.activation(h_relu[:, par, :], f_ps[:, D:D + FE], ACT.Relu).then_inc(relu_done, 1)

            def step(t, par):
                hi_of_transposes(t, par)
                if live(t + 1, TILES):
                    exps(t + 1, 1 - par, 1)
                if live(t + 2, TILES):
                    exps(t + 2, par, 0)
                if live(t - 1, TILES):
                    relu(t - 1, 1 - par)

            for g in range(H // 2):
                act.wait_ge(kt_ready, g + 1)
                act.activation(kt_sb[:, 2 * g:2 * g + 2, :].rearrange("p h n -> p (h n)"), s_ps[:, g, 0:2 * BK],
                               ACT.Copy, scale=SCALE2).then_inc(kt_copied, 1)
            for h in range(H):
                act.wait_ge(a_ready, h + 1)
                act.activation(a_hi[:, :, :, h * TK:(h + 1) * TK],
                               once_banks[h % 4][:, 0:DCH * BK].rearrange("p (c b k) -> p c b k", c=DCH, b=B),
                               ACT.Copy).then_inc(ahi_ready, 1)

            def stage_u(b):
                for g in range(H // 2):
                    act.wait_ge(u_ready, b * H // 2 + g + 1)
                    act.activation(u_stage[:, b, 2 * g:2 * g + 2, :].rearrange("p h d -> p (h d)"),
                                   once_banks[g][0:TK, 0:2 * D], ACT.Copy).then_inc(u_staged, 1)

            def hi_of_u(b):
                act.wait_ge(u_in[b], 32)
                act.activation(u_hi[:, b, 0:KC - 1, :], u_sb[:, b, 0:KC - 1, :], ACT.Copy)
                act.activation(u_hi[0:KLAST, b, KC - 1, :], u_sb[0:KLAST, b, KC - 1, :], ACT.Copy).then_inc(uhi_ready, 1)

            stage_u(0)
            exps(0, 0, 0)
            stage_u(1)
            exps(0, 0, 1)
            exps(1, 1, 0)
            hi_of_u(0)
            hi_of_u(1)
            step(0, 0)
            step(1, 1)
            pairs(act, 2, TILES - 2, step)
            for t in range(TILES - 2, TILES + 2):
                step(t, t % 2)

            act.wait_ge(gs, 2)
            act.activation(gap_e[:, :], gap_s[:, :], ACT.Exp).then_inc(gs, 1)
            act.wait_ge(gs, GATE_STEPS)
            any_open = act.value_load(flag[0:1, 0:1], min_val=0, max_val=1)
            with act.If(any_open > 0):
                with act.Fori(0, TILES) as t:
                    act.wait_ge(r_xt, t + 1)
                    act.activation(xnt, g_ps[:, 0:D].rearrange("p (c n) -> p c n", c=DCH), ACT.Copy).then_inc(r_xtc, 1)
                    act.wait_ge(r_h, t + 1)
                    for i in range(2):
                        a = act.activation(hr[:, 4 * i:4 * i + 4, :].rearrange("p e n -> p (e n)"), s_ps[:, i, :], ACT.Relu)
                    a.then_inc(r_relu, 1)

        @block.gpsimd
        def _(pool):
            def turned_x(t, par):
                if isinstance(t, int) and t % (2 * GB) == 0:
                    pool.wait_ge(xt_in[t // (2 * GB)], 32)
                if not isinstance(t, int) or t >= 2:
                    pool.wait_ge(s_ready, t - 1)
                src = xt_sb[:, :, par, bass.ds((t // 2) * P if isinstance(t, int) else block_col(t, par), P)]
                if isinstance(t, int) and t < 2:
                    pool.tensor_copy(xt_hi[:, par, :, :], src).then_inc(xthi_first, 1)
                    pool.wait_ge(xthi_first, t + 1)
                else:
                    pool.tensor_copy(xt_hi[:, par, :, :], src).then_inc(xthi_done, 1)
                    wait_apart(pool, xthi_done, t - 1)
                pool.tensor_tensor(xt_lo[:, par, :, :], src, xt_hi[:, par, :, :].bitcast(F32), ALU.subtract).then_inc(xt_ready, 1)

            def block_col(t, par):
                return (t - par) * (P // 2)

            def rstd_x(t, par):
                pool.wait_ge(var1_done, t + 1)
                pool.tensor_tensor(rstd1[:, par:par + 1], var1[:, par:par + 1], pow_neg[:, :], ALU.pow).then_inc(rstd1_done, 1)

            def normalise(t, par, half):
                pool.wait_ge(recip_ready, 2 * t + half + 1)
                rows = probs[:, par, half * HALF:(half + 1) * HALF].rearrange("p (h k) -> p h k", k=TK)
                hs = slice(half * H // 2, (half + 1) * H // 2)
                pool.tensor_tensor(rows, rows, recip[:, par, hs].unsqueeze(2).broadcast_to([P, H // 2, TK]),
                                   ALU.mult).then_inc(probs_ready, 1)

            def step(t, par):
                normalise(t, par, 0)
                if live(t + 2, TILES):
                    turned_x(t + 2, par)
                pool.tensor_tensor(xb_sb[:, par, :], x_sb[:, t, :], bo_sb[:, :], ALU.add).then_inc(xb_ready, 1)
                if not isinstance(t, int) or 1 <= t < TILES - 1:
                    rstd_x(t + 1, 1 - par)
                normalise(t, par, 1)

            pool.memset(ident[:, :], 0.0).then_inc(const_ready, 1)
            pool.memset(pow_neg[:, :], -0.5).then_inc(const_ready, 1)
            pool.memset(pow_pos[:, :], 0.5).then_inc(const_ready, 1)
            pool.wait_ge(const_ready, 3)
            pool.affine_select(out=ident[:, :], in_=ident[:, :], compare_op=ALU.not_equal, fill=1.0, base=0,
                               pattern=[[-1, P]], channel_multiplier=1).then_inc(const_ready, 1)
            turned_x(0, 0)
            turned_x(1, 1)
            rstd_x(0, 0)
            rstd_x(1, 1)
            pool.wait_ge(bo_in, 16)
            pool.wait_ge(x_in[0], 32)
            for i in range(1, 4):
                pool.wait_ge(xt_in[i], 32)
                pool.wait_ge(x_in[i], 32)
            step(0, 0)
            step(1, 1)
            pairs(pool, 2, TILES - 2, step)
            for t in range(TILES - 2, TILES):
                step(t, t % 2)
            pool.wait_ge(rvar2_done, TILES)
            pool.tensor_tensor(rstd2[:, :], rvar2[:, :], pow_pos[:, :], ALU.pow).then_inc(gs, 1)

        @block.vector
        def _(dve):
            def stats_x(t, par):
                dve.bn_stats(bn1[:, par, :], x_sb[:, t, :]).then_inc(bn1_done, 1)

            def aggregate_x(t, par):
                if isinstance(t, int):
                    dve.wait_ge(bn1_done, t + 1)
                dve.bn_aggr(mv1[:, par, :], bn1[:, par, :]).then_inc(mv1_done, 1)

            def variance_x(t, par):
                dve.wait_ge(mv1_done, t + 1)
                if not isinstance(t, int) or t >= 2:
                    dve.wait_ge(rstd1_done, t - 1)
                dve.tensor_scalar(var1[:, par:par + 1], mv1[:, par, 1:2], EPS, None, ALU.add).then_inc(var1_done, 1)

            def stats_x1(t, par):
                dve.wait_ge(x1_ready, t + 1)
                dve.bn_stats(bn2[:, par, :], x1_tr[:, par, :]).then_inc(bn2_done, 1)

            def aggregate_x1(t, par):
                wait_apart(dve, bn2_done, t + 1)
                dve.bn_aggr(mv2[:, par, :], bn2[:, par, :]).then_inc(mv2_done, 1)

            def variance_x1(t, par):
                dve.wait_ge(mv2_done, t + 1)
                dve.tensor_scalar(var2[:, par:par + 1], mv2[:, par, 1:2], EPS, None, ALU.add).then_inc(var2_done, 1)

            def rvar_x1(t, par):
                dve.wait_ge(var2_done, t + 1)
                dve.reciprocal(rvar2[:, bass.ds(t, 1)], var2[:, par:par + 1]).then_inc(rvar2_done, 1)

            def maxima(t, par):
                dve.wait_ge(s_ready, t + 1)
                dve.tensor_reduce(row_max[:, par, :].rearrange("p (i h) -> p i h", i=2),
                                  s_ps[:, 2 * par:2 * par + 2, 0:HALF].rearrange("p i (h k) -> p i h k", k=TK),
                                  X, ALU.max).then_inc(max_done, 1)

            def neg_maxima(t, par):
                dve.wait_ge(max_done, t + 1)
                dve.wait_ge(rstd1_done, t + 1)
                dve.tensor_scalar(neg_max[:, par, :], row_max[:, par, :], rstd1[:, par:par + 1], -1.0,
                                  ALU.mult, ALU.mult).then_inc(negmax_ready, 1)

            def reciprocals(t, par, half):
                dve.wait_ge(exp_done, 2 * t + half + 1)
                hs = slice(half * H // 2, (half + 1) * H // 2)
                dve.reciprocal(recip[:, par, hs], sums[:, par, hs]).then_inc(recip_ready, 1)

            def lo_of_transposes(t, par):
                if live(t, TILES):
                    dve.wait_ge(ghi_ready, 2 * t + 1)
                    dve.tensor_tensor(g_lo[:, 0:512], g_ps[:, 0:512], g_hi[:, 0:512].bitcast(F32),
                                      ALU.subtract).then_inc(glo_ready, 1)
                dve.wait_ge(ghi_ready, 2 * t + 2)
                lo, hi = second_bank(t)
                dve.tensor_tensor(g_lo[:, lo:hi], g_ps[:, lo:hi], g_hi[:, lo:hi].bitcast(F32),
                                  ALU.subtract).then_inc(glo_ready, 1 if live(t, TILES) else 2)

            def attended(t, par):
                dve.wait_ge(o_ready, t + 1)
                dve.wait_ge(xb_ready, t + 1)
                if not isinstance(t, int) or t >= 2:
                    dve.wait_ge(x1_kept, 8 * (t - par))
                dve.tensor_tensor(x1_tr[:, par, :], o_ps[:, 0:D], xb_sb[:, par, :], ALU.add).then_inc(x1_ready, 1)

            def squares(t, par):
                dve.wait_ge(relu_done, t + 1)
                dve.tensor_tensor(h2[:, par, :], h_relu[:, par, :], h_relu[:, par, :], ALU.mult).then_inc(h2_ready, 1)

            def top_logits(t, par):
                wait_apart(dve, hl_ready, t + 1)
                dve.max(top8[:, par, :], f_ps[:, D + FE:D + NL]).then_inc(top_done, 1)
                dve.tensor_copy(logits[:, t, :], f_ps[:, D + FE:D + NL]).then_inc(logits_done, 1)
                dve.wait_ge(top_done, t + 1)
                dve.tensor_tensor(gap[:, bass.ds(t, 1)], top8[:, par, 1:2], top8[:, par, 0:1], ALU.subtract)

            def result(t, par):
                dve.wait_ge(ffn_ready, t + 1)
                dve.wait_ge(rvar2_done, t + 1)
                dve.wait_ge(x1_kept, 8 * (t - par) + 16)
                dve.scalar_tensor_tensor(out=y_sb[:, t, :], in0=f_ps[:, 0:D], scalar=rvar2[:, bass.ds(t, 1)],
                                         in1=x1_sb[:, t, :], op0=ALU.mult, op1=ALU.add).then_inc(y_ready, 1)

            def step(t, par):
                if live(t + 1, TILES):
                    reciprocals(t + 1, 1 - par, 0)
                if live(t + 2, TILES):
                    stats_x(t + 2, par)
                if live(t - 1, TILES):
                    stats_x1(t - 1, 1 - par)
                if live(t - 1, TILES):
                    aggregate_x1(t - 1, 1 - par)
                if live(t + 2, TILES):
                    aggregate_x(t + 2, par)
                if live(t - 1, TILES):
                    variance_x1(t - 1, 1 - par)
                if live(t + 2, TILES):
                    variance_x(t + 2, par)
                if live(t - 1, TILES):
                    rvar_x1(t - 1, 1 - par)
                lo_of_transposes(t, par)
                if live(t + 2, TILES):
                    maxima(t + 2, par)
                if live(t + 1, TILES):
                    reciprocals(t + 1, 1 - par, 1)
                if live(t + 2, TILES):
                    neg_maxima(t + 2, par)
                if live(t, TILES):
                    attended(t, par)
                if live(t - 1, TILES):
                    squares(t - 1, 1 - par)
                    top_logits(t - 1, 1 - par)
                if live(t - 2, TILES):
                    result(t - 2, par)

            dve.memset(mean_of[:, :], 1.0 / D).then_inc(fill_ready, 1)
            dve.memset(probs[:, :, HK:KC * P], 0.0).then_inc(fill_ready, 1)
            dve.wait_ge(wmean_ready, 1)
            dve.tensor_tensor(wsr_c[:, :, :], wsr_sb[:, :, :],
                              f_ps[:, 0:NL].unsqueeze(1).broadcast_to([P, DCH, NL]), ALU.subtract).then_inc(wffn, 1)
            for i in range(2):
                hs = slice(i * H // 2, (i + 1) * H // 2)
                dve.wait_ge(wq_in[i], 16)
                dve.tensor_reduce(wq_mean[:, 0, hs], wqt_sb[:, hs, :], X, ALU.add).then_inc(wqs, 1)
                dve.wait_ge(wqs, 2 * i + 1)
                dve.tensor_scalar(wq_mean[:, 1, hs], wq_mean[:, 0, hs], 1.0 / D, None, ALU.mult).then_inc(wqs, 1)
                dve.wait_ge(wqs, 2 * i + 2)
                dve.tensor_tensor(wqt_sb[:, hs, :], wqt_sb[:, hs, :],
                                  wq_mean[:, 1, hs].unsqueeze(2).broadcast_to([P, H // 2, D]), ALU.subtract).then_inc(wq_ready, 1)
            for h in range(H):
                dve.wait_ge(ahi_ready, h + 1)
                at = (slice(None), slice(None), slice(None), slice(h * TK, (h + 1) * TK))
                dve.tensor_tensor(a_lo[at], once_banks[h % 4][:, 0:DCH * BK].rearrange("p (c b k) -> p c b k", c=DCH, b=B),
                                  a_hi[at].bitcast(F32), ALU.subtract).then_inc(alo_ready, 1)
            for g in range(H // 2):
                dve.wait_ge(vt_ready, g + 1)
                dve.tensor_copy(vt_sb[:, 2 * g:2 * g + 2, :].rearrange("p h n -> p (h n)"), s_ps[:, g, 0:2 * BK]).then_inc(vt_copied, 1)
            dve.wait_ge(x_in[0], 32)
            for t in range(2):
                stats_x(t, t)
                aggregate_x(t, t)
                variance_x(t, t)
            dve.wait_ge(wffn, 1)
            dve.tensor_copy(wsr_hi[:, :, :], wsr_c[:, :, :]).then_inc(wffn, 1)
            dve.wait_ge(ws2_in, 16)
            dve.tensor_copy(ws2_hi[:, :], ws2_sb[:, :]).then_inc(wffn, 1)
            dve.wait_ge(wffn, 3)
            dve.tensor_tensor(wsr_lo[:, :, :], wsr_c[:, :, :], wsr_hi[:, :, :].bitcast(F32), ALU.subtract).then_inc(wffn, 1)
            dve.tensor_tensor(ws2_lo[:, :], ws2_sb[:, :], ws2_hi[:, :].bitcast(F32), ALU.subtract).then_inc(wffn, 1)
            for t in range(2):
                maxima(t, t)
                neg_maxima(t, t)
            for half in range(2):
                reciprocals(0, 0, half)
            for b in range(B):
                dve.wait_ge(uhi_ready, b + 1)
                dve.tensor_tensor(u_lo[:, b, 0:KC - 1, :], u_sb[:, b, 0:KC - 1, :],
                                  u_hi[:, b, 0:KC - 1, :].bitcast(F32), ALU.subtract)
                dve.tensor_tensor(u_lo[0:KLAST, b, KC - 1, :], u_sb[0:KLAST, b, KC - 1, :],
                                  u_hi[0:KLAST, b, KC - 1, :].bitcast(F32), ALU.subtract).then_inc(ulo_ready, 1)
            for i in range(1, 4):
                dve.wait_ge(x_in[i], 32)
            step(0, 0)
            step(1, 1)
            pairs(dve, 2, TILES - 2, step)
            for t in range(TILES - 2, TILES + 2):
                step(t, t % 2)

            dve.wait_ge(gs, 1)
            dve.wait_ge(y_ready, TILES)
            dve.tensor_tensor(gap_s[:, :], gap[:, :], rstd2[:, :], ALU.mult).then_inc(gs, 1)
            dve.wait_ge(gs, 3)
            dve.tensor_scalar(gap_d[:, :], gap_e[:, :], 1.0, None, ALU.add).then_inc(gs, 1)
            dve.wait_ge(gs, 4)
            dve.tensor_scalar(gate[:, :], gap_d[:, :], 1.0, None, ALU.is_le).then_inc(gs, 1)
            dve.wait_ge(gs, 5)
            dve.tensor_reduce(gate_any[:, :], gate[:, :], X, ALU.max).then_inc(gs, 1)
            dve.wait_ge(gs, 7)
            dve.tensor_scalar(flag[:, :], o_ps[0:1, 0:1], 0.0, None, ALU.is_gt).then_inc(gs, 1)
            dve.wait_ge(gs, GATE_STEPS)
            any_open = dve.value_load(flag[0:1, 0:1], min_val=0, max_val=1)
            with dve.If(any_open > 0):
                with dve.Fori(0, TILES) as t:
                    dve.bn_stats(r_bn[:, :], x1_sb[:, t, :]).then_inc(r_dve, 1)
                    dve.tensor_reduce(gate_max[:, :], logits[:, t, :], X, ALU.max).then_inc(r_dve, 1)
                    dve.wait_ge(r_dve, 11 * t + 2)
                    dve.tensor_scalar(gate_e[:, :], logits[:, t, :], gate_max[:, 0:1], gate[:, bass.ds(t, 1)],
                                      ALU.is_equal, ALU.mult).then_inc(r_dve, 1)
                    dve.bn_aggr(r_mv[:, :], r_bn[:, :]).then_inc(r_dve, 1)
                    dve.wait_ge(r_dve, 11 * t + 4)
                    dve.tensor_scalar(xn, x1_sb[:, t, :], r_mv[:, 0:1], rstd2[:, bass.ds(t, 1)],
                                      ALU.subtract, ALU.mult).then_inc(r_x, 1)
                    dve.wait_ge(r_relu, t + 1)
                    dve.tensor_tensor(hr[:, :, :], hr[:, :, :], hr[:, :, :], ALU.mult).then_inc(r_hc, 1)
                    dve.wait_ge(r_y, t + 1)
                    for e in range(E):
                        acc = dve.scalar_tensor_tensor(
                            out=y_sb[:, t, :], in0=routed_banks[e // 2][:, (e % 2) * D:(e % 2 + 1) * D],
                            scalar=gate_e[:, e:e + 1], in1=y_sb[:, t, :], op0=ALU.mult, op1=ALU.add)
                        if e < E - 1:
                            acc.then_inc(r_dve, 1)
                            dve.wait_ge(r_dve, 11 * t + 5 + e)
                    acc.then_inc(r_acc, 1)

    return nc


def kernel(x, ctx_768, L0_xattn_Wq, L0_xattn_Wk, L0_xattn_Wv, L0_xattn_Wo, L0_xattn_bo,
           L0_ffn_Ws1, L0_ffn_Ws2, L0_ffn_W1, L0_ffn_W2, L0_ffn_Wr):
    import numpy as np
    from concourse import bacc
    from concourse.bass_utils import run_bass_kernel_spmd

    x = np.asarray(x)
    context = np.asarray(ctx_768)
    arrays = {
        "x": x,
        "x_t": x.reshape(-1, x.shape[-1]).T,
        "ctx_t": context.reshape(-1, context.shape[-1]).T,
        "wq_t": np.asarray(L0_xattn_Wq).T,
        "wk": L0_xattn_Wk, "wv": L0_xattn_Wv, "wo": L0_xattn_Wo, "bo": L0_xattn_bo,
        "ws1": L0_ffn_Ws1, "ws2": L0_ffn_Ws2, "w1": L0_ffn_W1, "w2": L0_ffn_W2, "wr": L0_ffn_Wr,
    }
    arrays = {f"in_{name}": np.ascontiguousarray(a) for name, a in arrays.items()}
    nc = bacc.Bacc("TRN2", target_bir_lowering=False, num_devices=1)
    ins = [nc.dram_tensor(name, a.shape, mybir.dt.from_np(a.dtype), kind="ExternalInput").ap() for name, a in arrays.items()]
    out = nc.dram_tensor("out", x.shape, mybir.dt.from_np(x.dtype), kind="ExternalOutput").ap()
    program(nc, *ins, out)
    result = run_bass_kernel_spmd(nc, [arrays], core_ids=[0])
    return result.results[0]["out"]
```

```python
from contextlib import ExitStack

import concourse.bass as bass
from concourse import mybir
from concourse.alu_op_type import AluOpType as ALU

F32 = mybir.dt.float32
F32R = mybir.dt.float32r
I32 = mybir.dt.int32
ACT = mybir.ActivationFunctionType
X = mybir.AxisListType.X

P = 128
EPS = 1e-5


def live(t, tiles):
    return not isinstance(t, int) or 0 <= t < tiles


def program(nc, x, x_t, ctx_t, wq_t, wk, wv, wo, bo, ws1, ws2, w1, w2, wr, out):
    B, TQ, D = x.shape
    TK = ctx_t.shape[1] // B
    DC = ctx_t.shape[0]
    H = wk.shape[1] // P
    E, _, FE = w1.shape
    DCH = D // P
    CP = DC // 2
    BK = B * TK
    HK = H * TK
    HALF = H // 2 * TK
    KC = -(-HK // P)
    KLAST = HK - (KC - 1) * P
    TILES = B * TQ // P
    NL = FE + E
    SCALE2 = float(P) ** -0.5
    assert B == 2 and FE == P and TILES % 4 == 0 and HALF <= 512 and KC == 5 and DCH == 2
    GATE_STEPS = 8
    PB = (KC - 1) * P
    XO = P
    HO = XO + D
    assert PB == 512 and HO + P == 512

    u_rows = nc.dram_tensor("u_rows", (B, HK, D), F32, kind="Internal").ap()

    with ExitStack() as ctx:
        def sb(name, shape, dt=F32):
            return ctx.enter_context(nc.sbuf_tensor(name, shape, dt))

        def psum(name, shape):
            return ctx.enter_context(nc.psum_tensor(name, shape, F32))

        def sem(name):
            return ctx.enter_context(nc.semaphore(name))

        ctx_sb = sb("ctx_sb", [CP, 2, BK])
        wk_sb = sb("wk_sb", [CP, 2, H * P])
        wv_sb = sb("wv_sb", [CP, 2, H * P])
        wqt_sb = sb("wqt_sb", [P, H, D])
        wq_mean = sb("wq_mean", [P, 2, H])
        wo_sb = sb("wo_sb", [P, H, D])
        kt_sb = sb("kt_sb", [P, H, BK])
        vt_sb = sb("vt_sb", [P, H, BK])
        a_hi = sb("a_hi", [P, DCH, B, HK], F32R)
        a_lo = sb("a_lo", [P, DCH, B, HK], F32R)
        u_stage = sb("u_stage", [TK, B, H, D])
        u_sb = sb("u_sb", [P, B, KC, D])
        u_hi = sb("u_hi", [P, B, KC - 1, D], F32R)
        u_lo = sb("u_lo", [P, B, KC - 1, D], F32R)
        bo_sb = sb("bo_sb", [P, D])
        wsr_sb = sb("wsr_sb", [P, DCH, NL])
        wsr_c = sb("wsr_c", [P, DCH, NL])
        ws2_sb = sb("ws2_sb", [P, D])
        ident = sb("ident", [P, P])
        mean_of = sb("mean_of", [P, P])
        pow_neg = sb("pow_neg", [P, 1])
        pow_pos = sb("pow_pos", [P, TILES])
        x_sb = sb("x_sb", [P, TILES, D])
        xt_sb = sb("xt_sb", [P, DCH, B, TQ])
        xb_sb = sb("xb_sb", [P, 2, D])
        x1_sb = sb("x1_sb", [P, TILES, D])
        y_sb = sb("y_sb", [P, TILES, D])
        xt_hi = sb("xt_hi", [P, 2, DCH, P], F32R)
        xt_lo = sb("xt_lo", [P, 2, DCH, P], F32R)
        probs = sb("probs", [P, 2, KC * P])
        pt_hi = sb("pt_hi", [P, PB], F32R)
        pt_lo = sb("pt_lo", [P, PB], F32R)
        g_sb = sb("g_sb", [P, HO + P])
        x1_tr = sb("x1_tr", [P, 2, D])
        h_relu = sb("h_relu", [P, 2, FE])
        h2 = sb("h2", [P, 2, FE])
        bn1 = sb("bn1", [P, 2, 6])
        bn2 = sb("bn2", [P, 2, 6])
        mv1 = sb("mv1", [P, 2, 2])
        mv2 = sb("mv2", [P, 2, 2])
        var1 = sb("var1", [P, 2])
        rstd1 = sb("rstd1", [P, 2])
        var2 = sb("var2", [P, 2])
        row_max = sb("row_max", [P, 2, H])
        neg_max = sb("neg_max", [P, 2, H])
        sums = sb("sums", [P, 2, H])
        recip = sb("recip", [P, 2, H])
        top8 = sb("top8", [P, 2, 8])
        rvar2 = sb("rvar2", [P, TILES])
        rstd2 = sb("rstd2", [P, TILES])
        logits = sb("logits", [P, TILES, E])
        gap = sb("gap", [P, TILES])
        gap_s = sb("gap_s", [P, TILES])
        gap_e = sb("gap_e", [P, TILES])
        gap_d = sb("gap_d", [P, TILES])
        gate = sb("gate", [P, TILES])
        gate_any = sb("gate_any", [P, 1])
        flag = sb("flag", [1, 1], I32)
        assert E == H and DCH * FE == D
        w1_sb = wqt_sb[:, :, :].rearrange("p e (c f) -> p e c f", c=DCH)
        w2_sb = wo_sb
        gate_e = sb("gate_e", [P, E])
        gate_max = sb("gate_max", [P, 1])
        r_bn = sb("r_bn", [P, 6])
        r_mv = sb("r_mv", [P, 2])
        xt_flat = xt_sb[:, 0, :, :].rearrange("p b n -> p (b n)")
        xn = x_sb[:, 0, :]
        xnt = x_sb[:, 1, :].rearrange("p (c n) -> p c n", c=DCH)
        hr = xt_flat[:, 0:E * P].rearrange("p (e n) -> p e n", e=E)

        s_ps = psum("s_ps", [P, 4, 512])
        g_ps = psum("g_ps", [P, 1024])
        o_ps = psum("o_ps", [P, 512])
        f_ps = psum("f_ps", [P, 512])
        routed_banks = [s_ps[:, 2, :], s_ps[:, 3, :], o_ps[:, :], f_ps[:, :]]
        once_banks = [g_ps[:, 0:512], g_ps[:, 512:1024], o_ps[:, :], f_ps[:, :]]

        ctx_in, wk_in, wsr_in, wv_in, wo_in, bo_in = (sem(n) for n in ("ctx_in", "wk_in", "wsr_in", "wv_in", "wo_in", "bo_in"))
        ws2_in = sem("ws2_in")
        wq_in = [sem(f"wq_in{i}") for i in range(2)]
        xt_in = [sem(f"xt_in{i}") for i in range(4)]
        x_in = [sem(f"x_in{i}") for i in range(4)]
        u_out = [sem(f"u_out{b}") for b in range(B)]
        u_in = [sem(f"u_in{b}") for b in range(B)]
        y_out = sem("y_out")
        w12_in = sem("w12_in")
        const_ready = sem("const_ready")
        fill_ready = sem("fill_ready")
        wmean_ready = sem("wmean_ready")
        kt_ready = sem("kt_ready")
        kt_copied = sem("kt_copied")
        vt_ready = sem("vt_ready")
        vt_copied = sem("vt_copied")
        wqs = sem("wqs")
        wq_ready = sem("wq_ready")
        a_ready = sem("a_ready")
        ahi_ready = sem("ahi_ready")
        alo_ready = sem("alo_ready")
        wsr_ready = sem("wsr_ready")
        u_ready = sem("u_ready")
        u_staged = [sem(f"u_staged{b}") for b in range(B)]
        uhi_ready = [sem(f"uhi_ready{b}") for b in range(B)]
        ulo_ready = [sem(f"ulo_ready{b}") for b in range(B)]
        bn1_done, mv1_done, var1_done = sem("bn1_done"), sem("mv1_done"), sem("var1_done")
        rstd1_done = sem("rstd1_done")
        xthi_first, xthi_done, xt_ready = sem("xthi_first"), sem("xthi_done"), sem("xt_ready")
        s_ready = sem("s_ready")
        max_done, negmax_ready = sem("max_done"), sem("negmax_ready")
        exp_done = sem("exp_done")
        recip_ready = sem("recip_ready")
        probs_ready = sem("probs_ready")
        xb_ready = sem("xb_ready")
        pt_done, g_done = sem("pt_done"), sem("g_done")
        pthi_ready, ptlo_ready = sem("pthi_ready"), sem("ptlo_ready")
        g_ready = sem("g_ready")
        o_ready = sem("o_ready")
        x1_ready = sem("x1_ready")
        x1_kept = sem("x1_kept")
        bn2_done, mv2_done, var2_done, rvar2_done = (sem(n) for n in ("bn2_done", "mv2_done", "var2_done", "rvar2_done"))
        f_ready = sem("f_ready")
        relu_done, h2_ready = sem("relu_done"), sem("h2_ready")
        top_done, logits_done = sem("top_done"), sem("logits_done")
        y_ready = sem("y_ready")
        gs = sem("gs")
        r_x, r_xt, r_xtc, r_h, r_hc, r_y, r_relu, r_acc, r_out, r_dve = (sem(n) for n in ("r_x", "r_xt", "r_xtc", "r_h", "r_hc", "r_y", "r_relu", "r_acc", "r_out", "r_dve"))

        def g_columns(t):
            if not isinstance(t, int):
                return 0, HO + P
            return (0 if t < TILES else XO if t == TILES else HO), (XO if t == 0 else HO if t == 1 else HO + P)

        x_rows = x.rearrange("b (n p) d -> p n b d", p=P)
        out_rows = out.rearrange("b (n p) d -> p n b d", p=P)
        xt_rows = x_t.rearrange("(c p) (b n) -> p c b n", p=P, b=B)
        y_pairs = y_sb[:, :, :].rearrange("p (n b) d -> p n b d", b=B)
        x_pairs = x_sb[:, :, :].rearrange("p (n b) d -> p n b d", b=B)
        NB = TQ // P
        GB = NB // 4

        def pairs(eng, first, last, step):
            with eng.Fori(first // 2, last // 2) as j:
                for par in range(2):
                    step(2 * j + par, par)

        def wait_apart(eng, semaphore, count):
            eng.wait_ge(const_ready, 4)
            eng.wait_ge(semaphore, count)

        block = ctx.enter_context(nc.Block())

        @block.sync
        def _(sp):
            sp.dma_start(ctx_sb[:, :, :], ctx_t.rearrange("(c p) n -> p c n", p=CP)).then_inc(ctx_in, 16)
            sp.dma_start(wv_sb[:, :, :], wv.rearrange("(c p) n -> p c n", p=CP)).then_inc(wv_in, 16)
            sp.dma_start(wo_sb[:, :, :], wo.rearrange("(h p) d -> p h d", p=P)).then_inc(wo_in, 16)
            sp.dma_start(wk_sb[:, :, :], wk.rearrange("(c p) n -> p c n", p=CP)).then_inc(wk_in, 16)
            for i in range(2):
                sp.dma_start(wqt_sb[:, i * H // 2:(i + 1) * H // 2, :],
                             wq_t.rearrange("(h p) d -> p h d", p=P)[:, i * H // 2:(i + 1) * H // 2, :]).then_inc(wq_in[i], 16)

            def load_x(i):
                for c in range(DCH):
                    sp.dma_start(xt_sb[:, c, :, i * GB * P:(i + 1) * GB * P],
                                 xt_rows[:, c, :, i * GB * P:(i + 1) * GB * P]).then_inc(xt_in[i], 16)
                for b in range(B):
                    sp.dma_start(x_pairs[:, i * GB:(i + 1) * GB, b, :], x_rows[:, i * GB:(i + 1) * GB, b, :]).then_inc(x_in[i], 16)

            load_x(0)
            sp.dma_start(wsr_sb[:, :, 0:FE], ws1.rearrange("(c p) f -> p c f", p=P)).then_inc(wsr_in, 16)
            sp.dma_start(wsr_sb[:, :, FE:NL], wr.rearrange("(c p) e -> p c e", p=P)).then_inc(wsr_in, 16)
            sp.dma_start(ws2_sb[:, :], ws2).then_inc(ws2_in, 16)
            sp.dma_start(bo_sb[:, :], bo.rearrange("(a d) -> a d", a=1).broadcast_to([P, D])).then_inc(bo_in, 16)
            for b in range(B):
                sp.wait_ge(u_staged[b], H // 2)
                sp.dma_start(u_rows[b].rearrange("(h k) d -> k h d", k=TK), u_stage[:, b, :, :]).then_inc(u_out[b], 16)
                if b == 0:
                    for i in range(1, 4):
                        load_x(i)
                sp.wait_ge(u_out[b], 16)
                sp.dma_start(u_sb[:, b, 0:KC - 1, :],
                             u_rows[b, 0:(KC - 1) * P, :].rearrange("(c p) d -> p c d", p=P)).then_inc(u_in[b], 16)
                sp.dma_start(u_sb[0:KLAST, b, KC - 1, :], u_rows[b, (KC - 1) * P:HK, :]).then_inc(u_in[b], 16)

            def keep_x1(k):
                sp.wait_ge(x1_ready, 2 * k + 2)
                sp.dma_start(x1_sb[:, bass.ds(2 * k, 2), :], x1_tr[:, :, :]).then_inc(x1_kept, 16)

            def store(k):
                sp.wait_ge(y_ready, 2 * k + 2)
                sp.dma_start(out_rows[:, k, :, :], y_sb[:, bass.ds(2 * k, 2), :]).then_inc(y_out, 16)

            keep_x1(0)
            with sp.Fori(1, NB) as k:
                keep_x1(k)
                store(k - 1)
            store(NB - 1)
            sp.wait_ge(y_out, 16 * NB)

            sp.wait_ge(gs, GATE_STEPS)
            any_open = sp.value_load(flag[0:1, 0:1], min_val=0, max_val=1)
            with sp.If(any_open > 0):
                sp.dma_start(w1_sb[:, :, :, :].rearrange("p e c f -> p (e c) f"),
                             w1.rearrange("e (c p) f -> p (e c) f", p=P)).then_inc(w12_in, 16)
                sp.dma_start(w2_sb[:, :, :], w2.rearrange("e p d -> p e d")).then_inc(w12_in, 16)
                with sp.Fori(0, NB) as k:
                    sp.wait_ge(r_acc, 2 * k + 2)
                    sp.dma_start(out_rows[:, k, :, :], y_sb[:, bass.ds(2 * k, 2), :]).then_inc(r_out, 16)
                sp.wait_ge(r_out, 16 * NB)

        @block.tensor
        def _(pe):
            def context_rows(w, ready, bank_free):
                for g in range(H // 2):
                    if bank_free is not None:
                        pe.wait_ge(bank_free, g + 1)
                    for h in (2 * g, 2 * g + 1):
                        for c in range(2):
                            mm = pe.matmul(s_ps[:, g, (h % 2) * BK:(h % 2 + 1) * BK], w[:, c, h * P:(h + 1) * P],
                                           ctx_sb[:, c, :], start=c == 0, stop=c == 1)
                    mm.then_inc(ready, 1)

            def make_a():
                for h in range(H):
                    pe.wait_ge(kt_copied, h // 2 + 1)
                    pe.wait_ge(wq_ready, h // (H // 2) + 1)
                    if h < 4:
                        pe.wait_ge(u_staged[0], h + 1)
                    else:
                        pe.wait_ge(alo_ready, h - 3)
                    for c in range(DCH):
                        mm = pe.matmul(once_banks[h % 4][:, c * BK:(c + 1) * BK], wqt_sb[:, h, c * P:(c + 1) * P],
                                       kt_sb[:, h, :], start=True, stop=True)
                    mm.then_inc(a_ready, 1)

            def make_u(b):
                for g in range(H // 2):
                    if b == 0:
                        pe.wait_ge(vt_copied, g + 1)
                    else:
                        pe.wait_ge(alo_ready, H - 3 + g)
                    for i in range(2):
                        h = 2 * g + i
                        mm = pe.matmul(once_banks[g][0:TK, i * D:(i + 1) * D], vt_sb[:, h, b * TK:(b + 1) * TK],
                                       wo_sb[:, h, :], start=True, stop=True)
                    mm.then_inc(u_ready, 1)

            def three(out_ap, hi, lo, rhs_hi, rhs_lo, first, last):
                pe.matmul(out_ap, hi, rhs_hi, start=first, stop=False)
                pe.matmul(out_ap, lo, rhs_hi, start=False, stop=False)
                return pe.matmul(out_ap, hi, rhs_lo, start=False, stop=last)

            def scores(t, par):
                pe.wait_ge(xt_ready, t + 1)
                if not isinstance(t, int) or t >= 2:
                    pe.wait_ge(exp_done, 2 * t - 2)
                for half in range(2):
                    if isinstance(t, int) and t == 0:
                        pe.wait_ge(alo_ready, (half + 1) * H // 2)
                    for c in range(DCH):
                        cols = slice(half * HALF, (half + 1) * HALF)
                        mm = three(s_ps[:, 2 * par + half, 0:HALF], xt_hi[:, par, c, :], xt_lo[:, par, c, :],
                                   a_hi[:, c, par, cols], a_lo[:, c, par, cols], c == 0, c == DCH - 1)
                mm.then_inc(s_ready, 1)

            def transposes(t, par):
                if live(t, TILES):
                    pe.wait_ge(probs_ready, 2 * t + 1)
                    for c in range(KC):
                        if (c + 1) * P > HALF and c * P <= HALF:
                            pe.wait_ge(probs_ready, 2 * t + 2)
                        to = g_ps[:, c * P:(c + 1) * P]
                        mm = pe.transpose(to, probs[:, par, c * P:(c + 1) * P], ident[:, :])
                        if c == KC - 2:
                            mm.then_inc(pt_done, 1)
                if live(t - 2, TILES):
                    pe.wait_ge(h2_ready, t - 1)
                    mm = pe.transpose(g_ps[:, PB + HO:PB + HO + P], h2[:, par, :], ident[:, :])
                if live(t - 1, TILES):
                    pe.wait_ge(x1_ready, t)
                    for c in range(DCH):
                        mm = pe.transpose(g_ps[:, PB + XO + c * P:PB + XO + (c + 1) * P],
                                          x1_tr[:, 1 - par, c * P:(c + 1) * P], ident[:, :])
                mm.then_inc(g_done, 1)

            def ffn(t, par):
                pe.wait_ge(g_ready, t + 1)
                if not isinstance(t, int) or t >= 2:
                    pe.wait_ge(logits_done, t - 1)
                if not isinstance(t, int) or t >= 3:
                    pe.wait_ge(y_ready, t - 2)
                if live(t - 2, TILES):
                    mm = pe.matmul(f_ps[:, 0:D], g_sb[:, HO:HO + P], ws2_sb[:, :], start=True, stop=True)
                if live(t - 1, TILES):
                    for c in range(DCH):
                        mm = pe.matmul(f_ps[:, D:D + NL], g_sb[:, XO + c * P:XO + (c + 1) * P], wsr_c[:, c, :],
                                       start=c == 0, stop=c == DCH - 1)
                mm.then_inc(f_ready, 1)

            def attention(t, par):
                if isinstance(t, int) and t < 2:
                    pe.wait_ge(uhi_ready[t], 1)
                    pe.wait_ge(ulo_ready[t], 1)
                pe.wait_ge(ptlo_ready, t + 1)
                for c in range(KC - 1):
                    three(o_ps[:, 0:D], pt_hi[:, c * P:(c + 1) * P], pt_lo[:, c * P:(c + 1) * P],
                          u_hi[:, par, c, :], u_lo[:, par, c, :], c == 0, False)
                pe.wait_ge(g_ready, t + 1)
                pe.matmul(o_ps[:, 0:D], g_sb[0:KLAST, 0:P], u_sb[0:KLAST, par, KC - 1, :],
                          start=False, stop=True).then_inc(o_ready, 1)

            def step(t, par):
                transposes(t, par)
                if live(t + 2, TILES):
                    scores(t + 2, par)
                if live(t - 1, TILES + 1):
                    ffn(t, par)
                if live(t, TILES):
                    attention(t, par)

            pe.wait_ge(ctx_in, 16)
            pe.wait_ge(wv_in, 16)
            context_rows(wv_sb, vt_ready, None)
            pe.wait_ge(wo_in, 16)
            make_u(0)
            pe.wait_ge(wk_in, 16)
            context_rows(wk_sb, kt_ready, vt_copied)
            make_a()
            scores(0, 0)
            make_u(1)
            scores(1, 1)
            pe.wait_ge(u_staged[1], H // 2)
            pe.wait_ge(const_ready, 4)
            pe.wait_ge(wsr_in, 32)
            pe.wait_ge(fill_ready, 2)
            for c in range(DCH):
                mm = pe.matmul(f_ps[:, 0:NL], mean_of[:, :], wsr_sb[:, c, :], start=c == 0, stop=c == DCH - 1)
            mm.then_inc(wmean_ready, 1)
            step(0, 0)
            pe.wait_ge(wsr_ready, 1)
            pe.wait_ge(ws2_in, 16)
            step(1, 1)
            pairs(pe, 2, TILES - 2, step)
            for t in range(TILES - 2, TILES + 2):
                step(t, t % 2)

            pe.wait_ge(gs, GATE_STEPS - 2)
            pe.matmul(o_ps[0:1, 0:1], gate_any[:, 0:1], mean_of[:, 0:1], start=True, stop=True).then_inc(gs, 1)
            pe.wait_ge(gs, GATE_STEPS)
            any_open = pe.value_load(flag[0:1, 0:1], min_val=0, max_val=1)
            with pe.If(any_open > 0):
                pe.wait_ge(w12_in, 32)
                with pe.Fori(0, TILES) as t:
                    pe.wait_ge(r_x, t + 1)
                    for c in range(DCH):
                        mm = pe.transpose(g_ps[:, c * P:(c + 1) * P], xn[:, c * P:(c + 1) * P], ident[:, :])
                    mm.then_inc(r_xt, 1)
                    pe.wait_ge(r_xtc, t + 1)
                    for e in range(E):
                        for c in range(DCH):
                            mm = pe.matmul(s_ps[:, e // 4, (e % 4) * P:(e % 4 + 1) * P], w1_sb[:, e, c, :], xnt[:, c, :],
                                           start=c == 0, stop=c == DCH - 1)
                    mm.then_inc(r_h, 1)
                    pe.wait_ge(r_hc, t + 1)
                    for e in range(E):
                        mm = pe.matmul(routed_banks[e // 2][:, (e % 2) * D:(e % 2 + 1) * D], hr[:, e, :], w2_sb[:, e, :],
                                       start=True, stop=True)
                    mm.then_inc(r_y, 1)

        @block.scalar
        def _(act):
            def copy_transposes(t, par):
                if live(t, TILES):
                    act.wait_ge(pt_done, t + 1)
                    act.activation(pt_hi[:, :], g_ps[:, 0:PB], ACT.Copy).then_inc(pthi_ready, 1)
                act.wait_ge(g_done, t + 1)
                lo, hi = g_columns(t)
                act.activation(g_sb[:, lo:hi], g_ps[:, PB + lo:PB + hi], ACT.Copy).then_inc(g_ready, 1)

            def exps(t, par, half):
                if half == 0:
                    act.wait_ge(negmax_ready, t + 1)
                for h in range(half * H // 2, (half + 1) * H // 2):
                    e = act.activation(probs[:, par, h * TK:(h + 1) * TK],
                                       s_ps[:, 2 * par + half, (h - half * H // 2) * TK:(h - half * H // 2 + 1) * TK],
                                       ACT.Exp, bias=neg_max[:, par, h:h + 1], scale=rstd1[:, par:par + 1],
                                       accum_out=sums[:, par, h:h + 1])
                e.then_inc(exp_done, 1)

            def relu(t, par):
                act.wait_ge(f_ready, t + 1)
                act.activation(h_relu[:, par, :], f_ps[:, D:D + FE], ACT.Relu).then_inc(relu_done, 1)

            def step(t, par):
                copy_transposes(t, par)
                if isinstance(t, int) and t == 0:
                    exps(1, 1, 0)
                if live(t + 1, TILES):
                    exps(t + 1, 1 - par, 1)
                if live(t - 1, TILES):
                    relu(t - 1, 1 - par)
                if live(t + 2, TILES):
                    exps(t + 2, par, 0)

            def hi_of_u(b):
                act.wait_ge(u_in[b], 32)
                act.activation(u_hi[:, b, :, :], u_sb[:, b, 0:KC - 1, :], ACT.Copy).then_inc(uhi_ready[b], 1)

            for g in range(H // 2):
                act.wait_ge(u_ready, g + 1)
                act.activation(u_stage[:, 0, 2 * g:2 * g + 2, :].rearrange("p h d -> p (h d)"),
                               once_banks[g][0:TK, 0:2 * D], ACT.Copy).then_inc(u_staged[0], 1)
            for g in range(H // 2):
                act.wait_ge(kt_ready, g + 1)
                act.activation(kt_sb[:, 2 * g:2 * g + 2, :].rearrange("p h n -> p (h n)"), s_ps[:, g, 0:2 * BK],
                               ACT.Copy, scale=SCALE2).then_inc(kt_copied, 1)
            for h in range(H):
                act.wait_ge(a_ready, h + 1)
                act.activation(a_hi[:, :, :, h * TK:(h + 1) * TK],
                               once_banks[h % 4][:, 0:DCH * BK].rearrange("p (c b k) -> p c b k", c=DCH, b=B),
                               ACT.Copy).then_inc(ahi_ready, 1)
            hi_of_u(0)
            exps(0, 0, 0)
            exps(0, 0, 1)
            step(0, 0)
            hi_of_u(1)
            step(1, 1)
            pairs(act, 2, TILES - 2, step)
            for t in range(TILES - 2, TILES + 2):
                step(t, t % 2)

            act.wait_ge(gs, 2)
            act.activation(gap_e[:, :], gap_s[:, :], ACT.Exp).then_inc(gs, 1)
            act.wait_ge(gs, GATE_STEPS)
            any_open = act.value_load(flag[0:1, 0:1], min_val=0, max_val=1)
            with act.If(any_open > 0):
                with act.Fori(0, TILES) as t:
                    act.wait_ge(r_xt, t + 1)
                    act.activation(xnt, g_ps[:, 0:D].rearrange("p (c n) -> p c n", c=DCH), ACT.Copy).then_inc(r_xtc, 1)
                    act.wait_ge(r_h, t + 1)
                    for i in range(2):
                        a = act.activation(hr[:, 4 * i:4 * i + 4, :].rearrange("p e n -> p (e n)"), s_ps[:, i, :], ACT.Relu)
                    a.then_inc(r_relu, 1)

        @block.gpsimd
        def _(pool):
            def turned_x(t, par):
                if isinstance(t, int) and t % (2 * GB) == 0:
                    pool.wait_ge(xt_in[t // (2 * GB)], 32)
                if not isinstance(t, int) or t >= 2:
                    pool.wait_ge(s_ready, t - 1)
                src = xt_sb[:, :, par, bass.ds((t // 2) * P if isinstance(t, int) else block_col(t, par), P)]
                if isinstance(t, int) and t < 2:
                    pool.tensor_copy(xt_hi[:, par, :, :], src).then_inc(xthi_first, 1)
                    pool.wait_ge(xthi_first, t + 1)
                else:
                    pool.tensor_copy(xt_hi[:, par, :, :], src).then_inc(xthi_done, 1)
                    wait_apart(pool, xthi_done, t - 1)
                pool.tensor_tensor(xt_lo[:, par, :, :], src, xt_hi[:, par, :, :].bitcast(F32), ALU.subtract).then_inc(xt_ready, 1)

            def block_col(t, par):
                return (t - par) * (P // 2)

            def rstd_x(t, par):
                pool.wait_ge(var1_done, t + 1)
                pool.tensor_tensor(rstd1[:, par:par + 1], var1[:, par:par + 1], pow_neg[:, :], ALU.pow).then_inc(rstd1_done, 1)

            def normalise(t, par, half):
                pool.wait_ge(recip_ready, 2 * t + half + 1)
                rows = probs[:, par, half * HALF:(half + 1) * HALF].rearrange("p (h k) -> p h k", k=TK)
                hs = slice(half * H // 2, (half + 1) * H // 2)
                pool.tensor_tensor(rows, rows, recip[:, par, hs].unsqueeze(2).broadcast_to([P, H // 2, TK]),
                                   ALU.mult).then_inc(probs_ready, 1)

            def step(t, par):
                normalise(t, par, 0)
                if live(t + 2, TILES):
                    turned_x(t + 2, par)
                if not isinstance(t, int) or 1 <= t < TILES - 1:
                    rstd_x(t + 1, 1 - par)
                normalise(t, par, 1)
                pool.tensor_tensor(xb_sb[:, par, :], x_sb[:, t, :], bo_sb[:, :], ALU.add).then_inc(xb_ready, 1)

            pool.memset(ident[:, :], 0.0).then_inc(const_ready, 1)
            pool.memset(pow_neg[:, :], -0.5).then_inc(const_ready, 1)
            pool.memset(pow_pos[:, :], 0.5).then_inc(const_ready, 1)
            pool.wait_ge(const_ready, 3)
            pool.affine_select(out=ident[:, :], in_=ident[:, :], compare_op=ALU.not_equal, fill=1.0, base=0,
                               pattern=[[-1, P]], channel_multiplier=1).then_inc(const_ready, 1)
            turned_x(0, 0)
            turned_x(1, 1)
            rstd_x(0, 0)
            rstd_x(1, 1)
            pool.wait_ge(uhi_ready[0], 1)
            pool.tensor_tensor(u_lo[:, 0, :, :], u_sb[:, 0, 0:KC - 1, :], u_hi[:, 0, :, :].bitcast(F32),
                               ALU.subtract).then_inc(ulo_ready[0], 1)
            pool.wait_ge(bo_in, 16)
            pool.wait_ge(x_in[0], 32)
            for i in range(1, 4):
                pool.wait_ge(xt_in[i], 32)
                pool.wait_ge(x_in[i], 32)
            step(0, 0)
            step(1, 1)
            pairs(pool, 2, TILES - 2, step)
            for t in range(TILES - 2, TILES):
                step(t, t % 2)
            pool.wait_ge(rvar2_done, TILES)
            pool.tensor_tensor(rstd2[:, :], rvar2[:, :], pow_pos[:, :], ALU.pow).then_inc(gs, 1)

        @block.vector
        def _(dve):
            def stats_x(t, par):
                dve.bn_stats(bn1[:, par, :], x_sb[:, t, :]).then_inc(bn1_done, 1)

            def aggregate_x(t, par):
                if isinstance(t, int):
                    dve.wait_ge(bn1_done, t + 1)
                dve.bn_aggr(mv1[:, par, :], bn1[:, par, :]).then_inc(mv1_done, 1)

            def variance_x(t, par):
                dve.wait_ge(mv1_done, t + 1)
                if not isinstance(t, int) or t >= 2:
                    dve.wait_ge(rstd1_done, t - 1)
                dve.tensor_scalar(var1[:, par:par + 1], mv1[:, par, 1:2], EPS, None, ALU.add).then_inc(var1_done, 1)

            def stats_x1(t, par):
                dve.wait_ge(x1_ready, t + 1)
                dve.bn_stats(bn2[:, par, :], x1_tr[:, par, :]).then_inc(bn2_done, 1)

            def aggregate_x1(t, par):
                wait_apart(dve, bn2_done, t + 1)
                dve.bn_aggr(mv2[:, par, :], bn2[:, par, :]).then_inc(mv2_done, 1)

            def variance_x1(t, par):
                dve.wait_ge(mv2_done, t + 1)
                dve.tensor_scalar(var2[:, par:par + 1], mv2[:, par, 1:2], EPS, None, ALU.add).then_inc(var2_done, 1)

            def rvar_x1(t, par):
                dve.wait_ge(var2_done, t + 1)
                dve.reciprocal(rvar2[:, bass.ds(t, 1)], var2[:, par:par + 1]).then_inc(rvar2_done, 1)

            def maxima(t, par):
                dve.wait_ge(s_ready, t + 1)
                dve.tensor_reduce(row_max[:, par, :].rearrange("p (i h) -> p i h", i=2),
                                  s_ps[:, 2 * par:2 * par + 2, 0:HALF].rearrange("p i (h k) -> p i h k", k=TK),
                                  X, ALU.max).then_inc(max_done, 1)

            def neg_maxima(t, par):
                dve.wait_ge(max_done, t + 1)
                dve.wait_ge(rstd1_done, t + 1)
                dve.tensor_scalar(neg_max[:, par, :], row_max[:, par, :], rstd1[:, par:par + 1], -1.0,
                                  ALU.mult, ALU.mult).then_inc(negmax_ready, 1)

            def reciprocals(t, par, half):
                dve.wait_ge(exp_done, 2 * t + half + 1)
                hs = slice(half * H // 2, (half + 1) * H // 2)
                dve.reciprocal(recip[:, par, hs], sums[:, par, hs]).then_inc(recip_ready, 1)

            def lo_of_transposes(t, par):
                dve.wait_ge(pthi_ready, t + 1)
                dve.tensor_tensor(pt_lo[:, :], g_ps[:, 0:PB], pt_hi[:, :].bitcast(F32),
                                  ALU.subtract).then_inc(ptlo_ready, 1)

            def attended(t, par):
                dve.wait_ge(o_ready, t + 1)
                dve.wait_ge(xb_ready, t + 1)
                if not isinstance(t, int) or t >= 2:
                    dve.wait_ge(x1_kept, 8 * (t - par))
                dve.tensor_tensor(x1_tr[:, par, :], o_ps[:, 0:D], xb_sb[:, par, :], ALU.add).then_inc(x1_ready, 1)

            def squares(t, par):
                dve.wait_ge(relu_done, t + 1)
                dve.tensor_tensor(h2[:, par, :], h_relu[:, par, :], h_relu[:, par, :], ALU.mult).then_inc(h2_ready, 1)

            def top_logits(t, par):
                wait_apart(dve, f_ready, t + 1)
                dve.max(top8[:, par, :], f_ps[:, D + FE:D + NL]).then_inc(top_done, 1)
                dve.tensor_copy(logits[:, t, :], f_ps[:, D + FE:D + NL]).then_inc(logits_done, 1)
                dve.wait_ge(top_done, t + 1)
                dve.tensor_tensor(gap[:, bass.ds(t, 1)], top8[:, par, 1:2], top8[:, par, 0:1], ALU.subtract)

            def result(t, par):
                dve.wait_ge(f_ready, t + 2)
                dve.wait_ge(rvar2_done, t + 1)
                dve.wait_ge(x1_kept, 8 * (t - par) + 16)
                dve.scalar_tensor_tensor(out=y_sb[:, t, :], in0=f_ps[:, 0:D], scalar=rvar2[:, bass.ds(t, 1)],
                                         in1=x1_sb[:, t, :], op0=ALU.mult, op1=ALU.add).then_inc(y_ready, 1)

            def step(t, par):
                if live(t, TILES):
                    lo_of_transposes(t, par)
                if live(t - 1, TILES):
                    stats_x1(t - 1, 1 - par)
                if live(t + 2, TILES):
                    aggregate_x(t + 2, par)
                if live(t - 1, TILES):
                    aggregate_x1(t - 1, 1 - par)
                if live(t + 2, TILES):
                    variance_x(t + 2, par)
                    maxima(t + 2, par)
                if isinstance(t, int) and t == 0:
                    reciprocals(1, 1, 0)
                if live(t + 1, TILES):
                    reciprocals(t + 1, 1 - par, 1)
                if live(t + 2, TILES):
                    neg_maxima(t + 2, par)
                if live(t - 1, TILES):
                    variance_x1(t - 1, 1 - par)
                    squares(t - 1, 1 - par)
                    rvar_x1(t - 1, 1 - par)
                    top_logits(t - 1, 1 - par)
                if live(t - 2, TILES):
                    result(t - 2, par)
                if live(t + 3, TILES):
                    stats_x(t + 3, 1 - par)
                if live(t, TILES):
                    attended(t, par)
                if live(t + 2, TILES):
                    reciprocals(t + 2, par, 0)

            dve.memset(mean_of[:, :], 1.0 / D).then_inc(fill_ready, 1)
            dve.memset(probs[:, :, HK:KC * P], 0.0).then_inc(fill_ready, 1)
            for g in range(H // 2):
                dve.wait_ge(vt_ready, g + 1)
                dve.tensor_copy(vt_sb[:, 2 * g:2 * g + 2, :].rearrange("p h n -> p (h n)"), s_ps[:, g, 0:2 * BK]).then_inc(vt_copied, 1)
            for i in range(2):
                hs = slice(i * H // 2, (i + 1) * H // 2)
                dve.wait_ge(wq_in[i], 16)
                dve.tensor_reduce(wq_mean[:, 0, hs], wqt_sb[:, hs, :], X, ALU.add).then_inc(wqs, 1)
                dve.wait_ge(wqs, 2 * i + 1)
                dve.tensor_scalar(wq_mean[:, 1, hs], wq_mean[:, 0, hs], 1.0 / D, None, ALU.mult).then_inc(wqs, 1)
                dve.wait_ge(wqs, 2 * i + 2)
                dve.tensor_tensor(wqt_sb[:, hs, :], wqt_sb[:, hs, :],
                                  wq_mean[:, 1, hs].unsqueeze(2).broadcast_to([P, H // 2, D]), ALU.subtract).then_inc(wq_ready, 1)
            dve.wait_ge(x_in[0], 32)
            for t in range(3):
                stats_x(t, t % 2)
                if t < 2:
                    aggregate_x(t, t)
                    variance_x(t, t)
            for h in range(H):
                dve.wait_ge(ahi_ready, h + 1)
                at = (slice(None), slice(None), slice(None), slice(h * TK, (h + 1) * TK))
                dve.tensor_tensor(a_lo[at], once_banks[h % 4][:, 0:DCH * BK].rearrange("p (c b k) -> p c b k", c=DCH, b=B),
                                  a_hi[at].bitcast(F32), ALU.subtract).then_inc(alo_ready, 1)
            maxima(0, 0)
            neg_maxima(0, 0)
            for g in range(H // 2):
                dve.wait_ge(u_ready, H // 2 + g + 1)
                dve.tensor_copy(u_stage[:, 1, 2 * g:2 * g + 2, :].rearrange("p h d -> p (h d)"),
                                once_banks[g][0:TK, 0:2 * D]).then_inc(u_staged[1], 1)
                if g >= 2:
                    reciprocals(0, 0, g - 2)
            maxima(1, 1)
            neg_maxima(1, 1)
            dve.wait_ge(wmean_ready, 1)
            dve.tensor_tensor(wsr_c[:, :, :], wsr_sb[:, :, :],
                              f_ps[:, 0:NL].unsqueeze(1).broadcast_to([P, DCH, NL]), ALU.subtract).then_inc(wsr_ready, 1)
            for i in range(1, 4):
                dve.wait_ge(x_in[i], 32)
            step(0, 0)
            dve.wait_ge(uhi_ready[1], 1)
            dve.tensor_tensor(u_lo[:, 1, :, :], u_sb[:, 1, 0:KC - 1, :], u_hi[:, 1, :, :].bitcast(F32),
                              ALU.subtract).then_inc(ulo_ready[1], 1)
            step(1, 1)
            pairs(dve, 2, TILES - 4, step)
            for t in range(TILES - 4, TILES + 2):
                step(t, t % 2)

            dve.wait_ge(gs, 1)
            dve.wait_ge(y_ready, TILES)
            dve.tensor_tensor(gap_s[:, :], gap[:, :], rstd2[:, :], ALU.mult).then_inc(gs, 1)
            dve.wait_ge(gs, 3)
            dve.tensor_scalar(gap_d[:, :], gap_e[:, :], 1.0, None, ALU.add).then_inc(gs, 1)
            dve.wait_ge(gs, 4)
            dve.tensor_scalar(gate[:, :], gap_d[:, :], 1.0, None, ALU.is_le).then_inc(gs, 1)
            dve.wait_ge(gs, 5)
            dve.tensor_reduce(gate_any[:, :], gate[:, :], X, ALU.max).then_inc(gs, 1)
            dve.wait_ge(gs, 7)
            dve.tensor_scalar(flag[:, :], o_ps[0:1, 0:1], 0.0, None, ALU.is_gt).then_inc(gs, 1)
            dve.wait_ge(gs, GATE_STEPS)
            any_open = dve.value_load(flag[0:1, 0:1], min_val=0, max_val=1)
            with dve.If(any_open > 0):
                with dve.Fori(0, TILES) as t:
                    dve.bn_stats(r_bn[:, :], x1_sb[:, t, :]).then_inc(r_dve, 1)
                    dve.tensor_reduce(gate_max[:, :], logits[:, t, :], X, ALU.max).then_inc(r_dve, 1)
                    dve.wait_ge(r_dve, 11 * t + 2)
                    dve.tensor_scalar(gate_e[:, :], logits[:, t, :], gate_max[:, 0:1], gate[:, bass.ds(t, 1)],
                                      ALU.is_equal, ALU.mult).then_inc(r_dve, 1)
                    dve.bn_aggr(r_mv[:, :], r_bn[:, :]).then_inc(r_dve, 1)
                    dve.wait_ge(r_dve, 11 * t + 4)
                    dve.tensor_scalar(xn, x1_sb[:, t, :], r_mv[:, 0:1], rstd2[:, bass.ds(t, 1)],
                                      ALU.subtract, ALU.mult).then_inc(r_x, 1)
                    dve.wait_ge(r_relu, t + 1)
                    dve.tensor_tensor(hr[:, :, :], hr[:, :, :], hr[:, :, :], ALU.mult).then_inc(r_hc, 1)
                    dve.wait_ge(r_y, t + 1)
                    for e in range(E):
                        acc = dve.scalar_tensor_tensor(
                            out=y_sb[:, t, :], in0=routed_banks[e // 2][:, (e % 2) * D:(e % 2 + 1) * D],
                            scalar=gate_e[:, e:e + 1], in1=y_sb[:, t, :], op0=ALU.mult, op1=ALU.add)
                        if e < E - 1:
                            acc.then_inc(r_dve, 1)
                            dve.wait_ge(r_dve, 11 * t + 5 + e)
                    acc.then_inc(r_acc, 1)

    return nc


def kernel(x, ctx_768, L0_xattn_Wq, L0_xattn_Wk, L0_xattn_Wv, L0_xattn_Wo, L0_xattn_bo,
           L0_ffn_Ws1, L0_ffn_Ws2, L0_ffn_W1, L0_ffn_W2, L0_ffn_Wr):
    import numpy as np
    from concourse import bacc
    from concourse.bass_utils import run_bass_kernel_spmd

    x = np.asarray(x)
    context = np.asarray(ctx_768)
    arrays = {
        "x": x,
        "x_t": x.reshape(-1, x.shape[-1]).T,
        "ctx_t": context.reshape(-1, context.shape[-1]).T,
        "wq_t": np.asarray(L0_xattn_Wq).T,
        "wk": L0_xattn_Wk, "wv": L0_xattn_Wv, "wo": L0_xattn_Wo, "bo": L0_xattn_bo,
        "ws1": L0_ffn_Ws1, "ws2": L0_ffn_Ws2, "w1": L0_ffn_W1, "w2": L0_ffn_W2, "wr": L0_ffn_Wr,
    }
    arrays = {f"in_{name}": np.ascontiguousarray(a) for name, a in arrays.items()}
    nc = bacc.Bacc("TRN2", target_bir_lowering=False, num_devices=1)
    ins = [nc.dram_tensor(name, a.shape, mybir.dt.from_np(a.dtype), kind="ExternalInput").ap() for name, a in arrays.items()]
    out = nc.dram_tensor("out", x.shape, mybir.dt.from_np(x.dtype), kind="ExternalOutput").ap()
    program(nc, *ins, out)
    result = run_bass_kernel_spmd(nc, [arrays], core_ids=[0])
    return result.results[0]["out"]
```

```python
from contextlib import ExitStack

import concourse.bass as bass
from concourse import mybir
from concourse.alu_op_type import AluOpType as ALU

F32 = mybir.dt.float32
F32R = mybir.dt.float32r
I32 = mybir.dt.int32
ACT = mybir.ActivationFunctionType
X = mybir.AxisListType.X

P = 128
EPS = 1e-5


def live(t, tiles):
    return not isinstance(t, int) or 0 <= t < tiles


def program(nc, x, x_t, ctx_t, wq_t, wk, wv, wo, bo, ws1, ws2, w1, w2, wr, out):
    B, TQ, D = x.shape
    TK = ctx_t.shape[1] // B
    DC = ctx_t.shape[0]
    H = wk.shape[1] // P
    E, _, FE = w1.shape
    DCH = D // P
    CP = DC // 2
    BK = B * TK
    HK = H * TK
    HALF = H // 2 * TK
    KC = -(-HK // P)
    KLAST = HK - (KC - 1) * P
    TILES = B * TQ // P
    TG = TILES // 4
    STATS = ((0, 2), (2, 2 * TG), (2 * TG, 3 * TG), (3 * TG, TILES))
    NL = FE + E
    SCALE2 = float(P) ** -0.5
    assert B == 2 and FE == P and TILES % 4 == 0 and HALF <= 512 and KC == 5 and DCH == 2
    GATE_STEPS = 9
    WARM_UP = 7
    WK_PARTS = ((0, H // 4), (H // 4, H // 2), (H // 2, H))
    PB = (KC - 1) * P
    XO = PB
    LO = XO + D
    HO = LO + P
    assert PB == 512 and HO + P == 1024

    with ExitStack() as ctx:
        def sb(name, shape, dt=F32):
            return ctx.enter_context(nc.sbuf_tensor(name, shape, dt))

        def psum(name, shape):
            return ctx.enter_context(nc.psum_tensor(name, shape, F32))

        def sem(name):
            return ctx.enter_context(nc.semaphore(name))

        ctx_sb = sb("ctx_sb", [CP, 2, BK])
        wqt_sb = sb("wqt_sb", [P, H, D])
        wq_mean = sb("wq_mean", [P, 2, H])
        wo_sb = sb("wo_sb", [P, H, D])
        kt_sb = sb("kt_sb", [P, H, BK])
        vt_hi = sb("vt_hi", [P, B, H * (P + TK) + P], F32R)
        vt_lo = sb("vt_lo", [P, B, H * (P + TK) + P], F32R)
        wo_hi = sb("wo_hi", [P, H, D], F32R)
        wo_lo = sb("wo_lo", [P, H, D], F32R)
        a_hi = sb("a_hi", [P, DCH, B, HK], F32R)
        a_lo = sb("a_lo", [P, DCH, B, HK], F32R)
        u_hi = sb("u_hi", [P, B, KC, D], F32R)
        u_lo = sb("u_lo", [P, B, KC, D], F32R)
        bo_sb = sb("bo_sb", [P, D])
        wsr_sb = sb("wsr_sb", [P, DCH, NL])
        wsr_c = sb("wsr_c", [P, DCH, NL])
        ws2_sb = sb("ws2_sb", [P, D])
        ws2_hi = sb("ws2_hi", [P, D], F32R)
        ws2_lo = sb("ws2_lo", [P, D], F32R)
        ident = sb("ident", [P, P])
        mean_of = sb("mean_of", [P, P])
        pow_neg = sb("pow_neg", [P, 2 * TG])
        bn1 = sb("bn1", [P, TILES, 6])
        mv1 = sb("mv1", [P, TILES, 2])
        var1 = sb("var1", [P, TILES])
        rstd1 = sb("rstd1", [P, TILES])
        pow_pos = sb("pow_pos", [P, TILES])
        x_sb = sb("x_sb", [P, TILES, D])
        xt_sb = sb("xt_sb", [P, DCH, B, TQ])
        xb_sb = sb("xb_sb", [P, 2, D])
        x1_sb = sb("x1_sb", [P, TILES, D])
        assert TILES == 2 * H and H * D == 2 * H * P
        wk_sb = x1_sb[0:CP, 0:H, :].rearrange("p (c e) d -> p c (e d)", c=2)
        wv_sb = x1_sb[0:CP, H:2 * H, :].rearrange("p (c e) d -> p c (e d)", c=2)
        y_sb = sb("y_sb", [P, TILES, D])
        xt_hi = sb("xt_hi", [P, 2, DCH, P], F32R)
        xt_lo = sb("xt_lo", [P, 2, DCH, P], F32R)
        probs = sb("probs", [P, 2, KC * P])
        pt_hi = sb("pt_hi", [P, KC * P + P], F32R)
        pt_lo = sb("pt_lo", [P, KC * P + P], F32R)
        g_sb = sb("g_sb", [P, D])
        g_last = sb("g_last", [P, D])
        x1_tr = sb("x1_tr", [P, 2, D])
        h_relu = sb("h_relu", [P, 2, FE])
        h2 = sb("h2", [P, 2, FE])
        bn2 = sb("bn2", [P, 2, 6])
        mv2 = sb("mv2", [P, 2, 2])
        var2 = sb("var2", [P, 2])
        row_max = sb("row_max", [P, 2, H])
        neg_max = sb("neg_max", [P, 2, H])
        sums = sb("sums", [P, 2, H])
        recip = sb("recip", [P, 2, H])
        top8 = sb("top8", [P, 2, 8])
        rvar2 = sb("rvar2", [P, TILES])
        rstd2 = sb("rstd2", [P, TILES])
        logits = sb("logits", [P, TILES, E])
        gap = sb("gap", [P, TILES])
        gap_s = sb("gap_s", [P, TILES])
        gap_e = sb("gap_e", [P, TILES])
        gap_d = sb("gap_d", [P, TILES])
        gate = sb("gate", [P, TILES])
        gate_any = sb("gate_any", [P, 1])
        flag = sb("flag", [1, 1], I32)
        assert E == H and DCH * FE == D
        w1_sb = wqt_sb[:, :, :].rearrange("p e (c f) -> p e c f", c=DCH)
        w2_sb = wo_sb
        gate_e = sb("gate_e", [P, E])
        gate_max = sb("gate_max", [P, 1])
        r_bn = sb("r_bn", [P, 6])
        r_mv = sb("r_mv", [P, 2])
        xt_flat = xt_sb[:, 0, :, :].rearrange("p b n -> p (b n)")
        xn = x_sb[:, 0, :]
        xnt = x_sb[:, 1, :].rearrange("p (c n) -> p c n", c=DCH)
        hr = xt_flat[:, 0:E * P].rearrange("p (e n) -> p e n", e=E)

        s_ps = psum("s_ps", [P, 4, 512])
        g_ps = psum("g_ps", [P, 1024])
        o_ps = psum("o_ps", [P, 512])
        f_ps = psum("f_ps", [P, 512])
        routed_banks = [s_ps[:, 2, :], s_ps[:, 3, :], o_ps[:, :], f_ps[:, :]]
        a_banks = [s_ps[:, i, :] for i in range(4)] + [g_ps[:, 0:512], g_ps[:, 512:1024], o_ps[:, :], f_ps[:, :]]
        once_banks = [g_ps[:, 0:512], g_ps[:, 512:1024], o_ps[:, :], f_ps[:, :]]

        ctx_in, wsr_in, wv_in, wo_in, bo_in = (sem(n) for n in ("ctx_in", "wsr_in", "wv_in", "wo_in", "bo_in"))
        wk_in = {heads[0]: sem(f"wk_in{heads[0]}") for heads in WK_PARTS}
        ws2_in = sem("ws2_in")
        wq_in = [sem(f"wq_in{i}") for i in range(2)]
        xt_in = [sem(f"xt_in{i}") for i in range(4)]
        x_in = [sem(f"x_in{i}") for i in range(4)]
        y_out = sem("y_out")
        w12_in = sem("w12_in")
        const_ready = sem("const_ready")
        fill_ready = sem("fill_ready")
        wmean_ready = sem("wmean_ready")
        ws2hi_ready, ws2lo_ready = sem("ws2hi_ready"), sem("ws2lo_ready")
        kt_ready = sem("kt_ready")
        kt_copied = sem("kt_copied")
        vt_ready = sem("vt_ready")
        vthi_ready, vtlo_ready = sem("vthi_ready"), sem("vtlo_ready")
        wohi_ready, wolo_ready = sem("wohi_ready"), sem("wolo_ready")
        wqs = sem("wqs")
        wq_ready = sem("wq_ready")
        a_ready = sem("a_ready")
        ahi_ready = sem("ahi_ready")
        alo_ready = sem("alo_ready")
        wsr_ready = sem("wsr_ready")
        u_ready = [sem(f"u_ready{b}") for b in range(B)]
        uhi_ready = [sem(f"uhi_ready{b}") for b in range(B)]
        ulo_ready = [sem(f"ulo_ready{b}") for b in range(B)]
        ulast_ready = sem("ulast_ready")
        ulasthi_ready = sem("ulasthi_ready")
        ulastlo_ready = sem("ulastlo_ready")
        bn1_done, mv1_done, var1_done = sem("bn1_done"), sem("mv1_done"), sem("var1_done")
        rstd1_done = sem("rstd1_done")
        xthi_first, xthi_done, xt_ready = sem("xthi_first"), sem("xthi_done"), sem("xt_ready")
        s_ready = sem("s_ready")
        max_done, negmax_ready = sem("max_done"), sem("negmax_ready")
        exp_done = sem("exp_done")
        recip_ready = sem("recip_ready")
        probs_ready = sem("probs_ready")
        xb_ready = sem("xb_ready")
        pt_done, g_done = sem("pt_done"), sem("g_done")
        pthi_ready, ptlo_ready = sem("pthi_ready"), sem("ptlo_ready")
        pthi_last, ptlo_last = sem("pthi_last"), sem("ptlo_last")
        g_ready = sem("g_ready")
        o_ready = sem("o_ready")
        x1_ready = sem("x1_ready")
        x1_kept = sem("x1_kept")
        bn2_done, mv2_done, var2_done, rvar2_done = (sem(n) for n in ("bn2_done", "mv2_done", "var2_done", "rvar2_done"))
        f_ready = sem("f_ready")
        last_ready = sem("last_ready")
        last_logits = sem("last_logits")
        relu_done, h2_ready = sem("relu_done"), sem("h2_ready")
        top_done, logits_done = sem("top_done"), sem("logits_done")
        gap_done = sem("gap_done")
        y_ready = sem("y_ready")
        gs = sem("gs")
        r_x, r_xt, r_xtc, r_h, r_hc, r_y, r_relu, r_acc, r_out, r_dve = (sem(n) for n in ("r_x", "r_xt", "r_xtc", "r_h", "r_hc", "r_y", "r_relu", "r_acc", "r_out", "r_dve"))

        def last_columns(t):
            return P if isinstance(t, int) and t < 2 else 2 * P

        LAST = TILES - 2

        def late(t):
            return isinstance(t, int) and t >= LAST

        def pt_bank(t, par, c):
            return s_ps[:, 2 * par, (c - 2) * P:(c - 1) * P] if late(t) and c >= 2 else g_ps[:, c * P:(c + 1) * P]

        def pt_count(t, pair):
            return LAST + 2 * (t - LAST) + pair + 1 if late(t) else t + 1

        x_rows = x.rearrange("b (n p) d -> p n b d", p=P)
        out_rows = out.rearrange("b (n p) d -> p n b d", p=P)
        xt_rows = x_t.rearrange("(c p) (b n) -> p c b n", p=P, b=B)
        y_pairs = y_sb[:, :, :].rearrange("p (n b) d -> p n b d", b=B)
        x_pairs = x_sb[:, :, :].rearrange("p (n b) d -> p n b d", b=B)
        NB = TQ // P
        GB = NB // 4

        def pairs(eng, first, last, step):
            with eng.Fori(first // 2, last // 2) as j:
                for par in range(2):
                    step(2 * j + par, par)

        def wait_apart(eng, semaphore, count):
            eng.wait_ge(const_ready, 4)
            eng.wait_ge(semaphore, count)

        def vt_heads(vt):
            return vt[:, :, 0:H * (P + TK)].rearrange("p b (h n) -> p h b n", h=H)

        block = ctx.enter_context(nc.Block())

        @block.sync
        def _(sp):
            sp.dma_start(ctx_sb[:, :, :], ctx_t.rearrange("(c p) n -> p c n", p=CP)).then_inc(ctx_in, 16)
            for heads in WK_PARTS:
                cols = slice(heads[0] * P, heads[1] * P)
                sp.dma_start(wk_sb[:, :, cols], wk.rearrange("(c p) n -> p c n", p=CP)[:, :, cols]).then_inc(wk_in[heads[0]], 16)
            sp.dma_start(wv_sb[:, :, :], wv.rearrange("(c p) n -> p c n", p=CP)).then_inc(wv_in, 16)
            for i in range(2):
                sp.dma_start(wqt_sb[:, i * H // 2:(i + 1) * H // 2, :],
                             wq_t.rearrange("(h p) d -> p h d", p=P)[:, i * H // 2:(i + 1) * H // 2, :]).then_inc(wq_in[i], 16)

            def load_x_t(i):
                for c in range(DCH):
                    sp.dma_start(xt_sb[:, c, :, i * GB * P:(i + 1) * GB * P],
                                 xt_rows[:, c, :, i * GB * P:(i + 1) * GB * P]).then_inc(xt_in[i], 16)

            def load_x(i):
                for b in range(B):
                    sp.dma_start(x_pairs[:, i * GB:(i + 1) * GB, b, :], x_rows[:, i * GB:(i + 1) * GB, b, :]).then_inc(x_in[i], 16)

            load_x_t(0)
            sp.dma_start(wo_sb[:, :, :], wo.rearrange("(h p) d -> p h d", p=P)).then_inc(wo_in, 16)
            load_x(0)
            sp.dma_start(wsr_sb[:, :, 0:FE], ws1.rearrange("(c p) f -> p c f", p=P)).then_inc(wsr_in, 16)
            sp.dma_start(wsr_sb[:, :, FE:NL], wr.rearrange("(c p) e -> p c e", p=P)).then_inc(wsr_in, 16)
            sp.dma_start(bo_sb[:, :], bo.rearrange("(a d) -> a d", a=1).broadcast_to([P, D])).then_inc(bo_in, 16)
            sp.dma_start(ws2_sb[:, :], ws2).then_inc(ws2_in, 16)
            for i in range(1, 4):
                load_x_t(i)
                load_x(i)

            def keep_x1(k):
                sp.wait_ge(x1_ready, 2 * k + 2)
                sp.dma_start(x1_sb[:, bass.ds(2 * k, 2), :], x1_tr[:, :, :]).then_inc(x1_kept, 16)

            def store(k):
                sp.wait_ge(y_ready, 2 * k + 2)
                sp.dma_start(out_rows[:, k, :, :], y_sb[:, bass.ds(2 * k, 2), :]).then_inc(y_out, 16)

            keep_x1(0)
            with sp.Fori(1, NB) as k:
                keep_x1(k)
                store(k - 1)
            for b in range(B):
                sp.wait_ge(y_ready, 2 * (NB - 1) + b + 1)
                sp.dma_start(out_rows[:, NB - 1, b, :], y_sb[:, 2 * (NB - 1) + b, :]).then_inc(y_out, 16)
            sp.wait_ge(y_out, 16 * (NB + 1))

            sp.wait_ge(gs, GATE_STEPS)
            any_open = sp.value_load(flag[0:1, 0:1], min_val=0, max_val=1)
            with sp.If(any_open > 0):
                sp.dma_start(w1_sb[:, :, :, :].rearrange("p e c f -> p (e c) f"),
                             w1.rearrange("e (c p) f -> p (e c) f", p=P)).then_inc(w12_in, 16)
                sp.dma_start(w2_sb[:, :, :], w2.rearrange("e p d -> p e d")).then_inc(w12_in, 16)
                with sp.Fori(0, NB) as k:
                    sp.wait_ge(r_acc, 2 * k + 2)
                    sp.dma_start(out_rows[:, k, :, :], y_sb[:, bass.ds(2 * k, 2), :]).then_inc(r_out, 16)
                sp.wait_ge(r_out, 16 * NB)

        @block.tensor
        def _(pe):
            def context_rows(w, w_in, banks, ready):
                for g in range(H // 2):
                    if 2 * g in w_in:
                        pe.wait_ge(w_in[2 * g], 16)
                    for h in (2 * g, 2 * g + 1):
                        for c in range(2):
                            mm = pe.matmul(banks[g][:, (h % 2) * BK:(h % 2 + 1) * BK], w[:, c, h * P:(h + 1) * P],
                                           ctx_sb[:, c, :], start=c == 0, stop=c == 1)
                    mm.then_inc(ready, 1)

            def make_a():
                for h in range(H):
                    pe.wait_ge(wq_ready, h // (H // 2) + 1)
                    if h < 4:
                        pe.wait_ge(kt_copied, h + 1)
                    else:
                        pe.wait_ge(vtlo_ready, h - 3)
                    for c in range(DCH):
                        mm = pe.matmul(a_banks[h][:, c * BK:(c + 1) * BK], wqt_sb[:, h, c * P:(c + 1) * P],
                                       kt_sb[:, h, :], start=True, stop=True)
                    mm.then_inc(a_ready, 1)

            def three(out_ap, hi, lo, rhs_hi, rhs_lo, first, last):
                pe.matmul(out_ap, hi, rhs_hi, start=first, stop=False)
                pe.matmul(out_ap, lo, rhs_hi, start=False, stop=False)
                return pe.matmul(out_ap, hi, rhs_lo, start=False, stop=last)

            def u_chunk(b, c, to):
                rows = P if c < KC - 1 else KLAST
                heads = [h for h in range(H) if h * TK < c * P + rows and (h + 1) * TK > c * P]
                for h in heads:
                    if b == 0:
                        pe.wait_ge(wolo_ready, h // 2 + 1)
                    at = slice((c + h + 1) * P, (c + h + 1) * P + rows)
                    mm = three(to[0:rows, :], vt_hi[:, b, at], vt_lo[:, b, at], wo_hi[:, h, :], wo_lo[:, h, :],
                               h == heads[0], h == heads[-1])
                return mm

            def make_u(b, i, bank):
                for c in (2 * i, 2 * i + 1):
                    mm = u_chunk(b, c, bank[:, (c % 2) * D:(c % 2 + 1) * D])
                mm.then_inc(u_ready[b], 1)

            def scores(t, par, parts=((0, 0), (0, 1), (1, 0), (1, 1))):
                if parts[0] == (0, 0):
                    pe.wait_ge(xt_ready, t + 1)
                    if not isinstance(t, int) or t >= 2:
                        pe.wait_ge(exp_done, 2 * t - 2)
                for half, c in parts:
                    if isinstance(t, int) and t == 0 and c == 0:
                        pe.wait_ge(alo_ready, (half + 1) * H // 2)
                    cols = slice(half * HALF, (half + 1) * HALF)
                    mm = three(s_ps[:, 2 * par + half, 0:HALF], xt_hi[:, par, c, :], xt_lo[:, par, c, :],
                               a_hi[:, c, par, cols], a_lo[:, c, par, cols], c == 0, c == DCH - 1)
                if parts[-1] == (1, 1):
                    mm.then_inc(s_ready, 1)

            def transposes(t, par):
                if live(t, TILES):
                    pe.wait_ge(probs_ready, 2 * t + 1)
                    for c in range(KC):
                        if (c + 1) * P > HALF and c * P <= HALF:
                            pe.wait_ge(probs_ready, 2 * t + 2)
                        to = pt_bank(t, par, c) if c < KC - 1 else g_ps[:, LO:LO + P]
                        mm = pe.transpose(to, probs[:, par, c * P:(c + 1) * P], ident[:, :])
                        if c == KC - 2 or (late(t) and c == 1):
                            mm.then_inc(pt_done, 1)
                if live(t - 2, TILES):
                    pe.wait_ge(h2_ready, t - 1)
                    mm = pe.transpose(g_ps[:, HO:HO + P], h2[:, par, :], ident[:, :])
                return mm

            def transposes_x1(t, par, mm):
                if live(t - 1, TILES):
                    pe.wait_ge(x1_ready, t)
                    for c in range(DCH):
                        mm = pe.transpose(g_ps[:, XO + c * P:XO + (c + 1) * P],
                                          x1_tr[:, 1 - par, c * P:(c + 1) * P], ident[:, :])
                mm.then_inc(g_done, 1)

            def ffn_rows(t):
                pe.wait_ge(ptlo_last, t + 1)
                return three(f_ps[:, 0:D], pt_hi[:, KC * P:], pt_lo[:, KC * P:], ws2_hi[:, :], ws2_lo[:, :], True, True)

            def ffn(t, par):
                pe.wait_ge(g_ready, t)
                if not isinstance(t, int) or t >= 2:
                    pe.wait_ge(logits_done, t - 1)
                if not isinstance(t, int) or t >= 3:
                    pe.wait_ge(y_ready, t - 2)
                for c in range(DCH):
                    mm = pe.matmul(f_ps[:, D:D + NL], g_sb[:, c * P:(c + 1) * P], wsr_c[:, c, :],
                                   start=c == 0, stop=c == DCH - 1)
                if live(t - 2, TILES):
                    mm = ffn_rows(t)
                mm.then_inc(f_ready, 1)

            def attention(t, par):
                if isinstance(t, int) and t < 2:
                    pe.wait_ge(ulo_ready[t], 2)
                    if t == 0:
                        pe.wait_ge(ulo_ready[1], 2)
                        pe.wait_ge(ulastlo_ready, 1)
                pe.wait_ge(ptlo_ready, pt_count(t, 0))
                for c in range(KC):
                    if c == 2 and late(t):
                        pe.wait_ge(ptlo_ready, pt_count(t, 1))
                    if c == KC - 1:
                        pe.wait_ge(ptlo_last, t + 1)
                    k = slice(0, P if c < KC - 1 else KLAST)
                    mm = three(o_ps[:, 0:D], pt_hi[k, c * P:(c + 1) * P], pt_lo[k, c * P:(c + 1) * P],
                               u_hi[k, par, c, :], u_lo[k, par, c, :], c == 0, c == KC - 1)
                mm.then_inc(o_ready, 1)

            def step(t, par):
                mm = transposes(t, par)
                if live(t + 2, TILES) and live(t - 1, TILES):
                    scores(t + 2, par, ((0, 0),))
                    transposes_x1(t, par, mm)
                    scores(t + 2, par, ((0, 1), (1, 0), (1, 1)))
                else:
                    transposes_x1(t, par, mm)
                    if live(t + 2, TILES):
                        scores(t + 2, par)
                if live(t - 1, TILES):
                    ffn(t, par)
                attention(t, par)

            pe.wait_ge(fill_ready, 1)
            for _ in range(WARM_UP):
                pe.matmul(f_ps[:, 0:P], mean_of[:, :], mean_of[:, :], start=True, stop=True)
            pe.wait_ge(ctx_in, 16)
            context_rows(wk_sb, wk_in, [s_ps[:, g, :] for g in range(4)], kt_ready)
            context_rows(wv_sb, {0: wv_in}, once_banks, vt_ready)
            make_a()
            scores(0, 0, ((0, 0), (0, 1)))
            pe.wait_ge(wsr_in, 32)
            pe.wait_ge(fill_ready, 4)
            for c in range(DCH):
                mm = pe.matmul(s_ps[:, 2, 0:NL], mean_of[:, :], wsr_sb[:, c, :], start=c == 0, stop=c == DCH - 1)
            mm.then_inc(wmean_ready, 1)
            scores(0, 0, ((1, 0), (1, 1)))
            pe.wait_ge(wsr_ready, 1)
            scores(1, 1)
            make_u(0, 0, g_ps[:, 0:512])
            make_u(0, 1, g_ps[:, 512:1024])
            for b in range(B):
                mm = u_chunk(b, KC - 1, f_ps[:, b * D:(b + 1) * D])
            mm.then_inc(ulast_ready, 1)
            pe.wait_ge(ulo_ready[0], 1)
            make_u(1, 0, g_ps[:, 0:512])
            make_u(1, 1, o_ps)
            pe.wait_ge(const_ready, 4)
            pe.wait_ge(ulo_ready[0], 2)
            pe.wait_ge(ulo_ready[1], 1)
            step(0, 0)
            step(1, 1)
            pe.wait_ge(ws2lo_ready, 1)
            pairs(pe, 2, TILES - 2, step)
            def turned_hidden(to, x1_t):
                for c in range(DCH):
                    mm = pe.matmul(to, wsr_c[:, c, 0:FE], x1_t[:, c * P:(c + 1) * P], start=c == 0, stop=c == DCH - 1)
                mm.then_inc(f_ready, 1)

            def late_logits(t, x1_t):
                for c in range(DCH):
                    mm = pe.matmul(s_ps[:, 2 * (t % 2) + 1, 0:E], x1_t[:, c * P:(c + 1) * P], wsr_c[:, c, FE:NL],
                                   start=c == 0, stop=c == DCH - 1)
                mm.then_inc(last_logits, 1)

            def late_rows(t):
                pe.wait_ge(h2_ready, t + 1)
                pe.matmul(s_ps[:, 2 * (t % 2), 0:D], h2[:, t % 2, :], ws2_sb[:, :], start=True, stop=True).then_inc(last_ready, 1)

            transposes_x1(LAST, 0, transposes(LAST, 0))
            attention(LAST, 0)
            ffn(LAST, 0)
            transposes_x1(LAST + 1, 1, transposes(LAST + 1, 1))
            attention(LAST + 1, 1)
            pe.wait_ge(g_ready, LAST + 1)
            pe.wait_ge(logits_done, LAST)
            pe.wait_ge(y_ready, LAST - 1)
            ffn_rows(LAST + 1)
            turned_hidden(f_ps[:, D:D + P], g_sb)
            transposes_x1(TILES, 0, None)
            late_logits(LAST, g_sb)
            pe.wait_ge(g_ready, TILES)
            turned_hidden(o_ps[:, 0:P], g_last)
            late_rows(LAST)
            late_rows(LAST + 1)
            late_logits(LAST + 1, g_last)

            pe.wait_ge(gs, GATE_STEPS - 2)
            pe.matmul(o_ps[0:1, 0:1], gate_any[:, 0:1], mean_of[:, 0:1], start=True, stop=True).then_inc(gs, 1)
            pe.wait_ge(gs, GATE_STEPS)
            any_open = pe.value_load(flag[0:1, 0:1], min_val=0, max_val=1)
            with pe.If(any_open > 0):
                pe.wait_ge(w12_in, 32)
                with pe.Fori(0, TILES) as t:
                    pe.wait_ge(r_x, t + 1)
                    for c in range(DCH):
                        mm = pe.transpose(g_ps[:, c * P:(c + 1) * P], xn[:, c * P:(c + 1) * P], ident[:, :])
                    mm.then_inc(r_xt, 1)
                    pe.wait_ge(r_xtc, t + 1)
                    for e in range(E):
                        for c in range(DCH):
                            mm = pe.matmul(s_ps[:, e // 4, (e % 4) * P:(e % 4 + 1) * P], w1_sb[:, e, c, :], xnt[:, c, :],
                                           start=c == 0, stop=c == DCH - 1)
                    mm.then_inc(r_h, 1)
                    pe.wait_ge(r_hc, t + 1)
                    for e in range(E):
                        mm = pe.matmul(routed_banks[e // 2][:, (e % 2) * D:(e % 2 + 1) * D], hr[:, e, :], w2_sb[:, e, :],
                                       start=True, stop=True)
                    mm.then_inc(r_y, 1)

        @block.scalar
        def _(act):
            def copy_transposes(t, par):
                if late(t) and t < TILES:
                    for pair in range(2):
                        act.wait_ge(pt_done, pt_count(t, pair))
                        act.activation(pt_hi[:, 2 * pair * P:2 * (pair + 1) * P], (g_ps[:, 0:2 * P], s_ps[:, 2 * par, 0:2 * P])[pair],
                                       ACT.Copy).then_inc(pthi_ready, 1)
                elif live(t, TILES):
                    act.wait_ge(pt_done, t + 1)
                    act.activation(pt_hi[:, 0:PB], g_ps[:, 0:PB], ACT.Copy).then_inc(pthi_ready, 1)
                act.wait_ge(g_done, t + 1)
                if isinstance(t, int) and t == TILES:
                    act.activation(g_last[:, :], g_ps[:, XO:XO + D], ACT.Copy).then_inc(g_ready, 1)
                elif live(t - 1, TILES):
                    act.activation(g_sb[:, :], g_ps[:, XO:XO + D], ACT.Copy).then_inc(g_ready, 1)
                if live(t, TILES):
                    n = last_columns(t)
                    act.activation(pt_hi[:, PB:PB + n], g_ps[:, LO:LO + n], ACT.Copy).then_inc(pthi_last, 1)

            def exps(t, par, half):
                if half == 0:
                    act.wait_ge(negmax_ready, t + 1)
                for h in range(half * H // 2, (half + 1) * H // 2):
                    e = act.activation(probs[:, par, h * TK:(h + 1) * TK],
                                       s_ps[:, 2 * par + half, (h - half * H // 2) * TK:(h - half * H // 2 + 1) * TK],
                                       ACT.Exp, bias=neg_max[:, par, h:h + 1], scale=rstd1[:, bass.ds(t, 1)],
                                       accum_out=sums[:, par, h:h + 1])
                e.then_inc(exp_done, 1)

            def relu(t, par):
                act.wait_ge(f_ready, t + 1)
                units = o_ps[:, 0:P] if isinstance(t, int) and t == TILES - 1 else f_ps[:, D:D + FE]
                act.activation(h_relu[:, par, :], units, ACT.Relu).then_inc(relu_done, 1)

            def step(t, par):
                copy_transposes(t, par)
                if live(t + 1, TILES):
                    exps(t + 1, 1 - par, 1)
                if live(t - 1, TILES):
                    relu(t - 1, 1 - par)
                if live(t + 2, TILES):
                    exps(t + 2, par, 0)

            def hi_of_u(b, i, bank):
                act.wait_ge(u_ready[b], i + 1)
                act.activation(u_hi[:, b, 2 * i:2 * i + 2, :].rearrange("p c d -> p (c d)"), bank[:, :], ACT.Copy).then_inc(uhi_ready[b], 1)

            for g in range(H // 2):
                act.wait_ge(kt_ready, g + 1)
                act.activation(kt_sb[:, 2 * g:2 * g + 2, :].rearrange("p h n -> p (h n)"), s_ps[:, g, 0:2 * BK],
                               ACT.Copy, scale=SCALE2).then_inc(kt_copied, 1)
            act.wait_ge(fill_ready, 3)
            for g in range(H // 2):
                act.wait_ge(vt_ready, g + 1)
                for h in (2 * g, 2 * g + 1):
                    v = act.activation(vt_heads(vt_hi)[:, h, :, P:P + TK],
                                       once_banks[g][:, (h % 2) * BK:(h % 2 + 1) * BK].rearrange("p (b n) -> p b n", b=B), ACT.Copy)
                v.then_inc(vthi_ready, 1)
            for h in range(H):
                act.wait_ge(a_ready, h + 1)
                act.activation(a_hi[:, :, :, h * TK:(h + 1) * TK],
                               a_banks[h][:, 0:DCH * BK].rearrange("p (c b k) -> p c b k", c=DCH, b=B),
                               ACT.Copy).then_inc(ahi_ready, 1)
                for q in {H // 2 - 1: (0,), H // 2: (1,), H - 1: (2, 3)}.get(h, ()):
                    hs = slice(2 * q, 2 * q + 2)
                    act.wait_ge(wo_in, 16)
                    act.activation(wo_hi[:, hs, :], wo_sb[:, hs, :], ACT.Copy).then_inc(wohi_ready, 1)
            act.wait_ge(ws2_in, 16)
            act.activation(ws2_hi[:, :], ws2_sb[:, :], ACT.Copy).then_inc(ws2hi_ready, 1)
            exps(0, 0, 0)
            exps(0, 0, 1)
            hi_of_u(0, 0, g_ps[:, 0:512])
            hi_of_u(0, 1, g_ps[:, 512:1024])
            exps(1, 1, 0)
            act.wait_ge(ulast_ready, 1)
            act.activation(u_hi[0:KLAST, :, KC - 1, :], f_ps[0:KLAST, :].rearrange("p (b d) -> p b d", b=B),
                           ACT.Copy).then_inc(ulasthi_ready, 1)
            hi_of_u(1, 0, g_ps[:, 0:512])
            hi_of_u(1, 1, o_ps)
            step(0, 0)
            step(1, 1)
            pairs(act, 2, TILES - 2, step)
            for t in range(TILES - 2, TILES + 1):
                step(t, t % 2)

            act.wait_ge(gs, 3)
            act.activation(gap_e[:, :], gap_s[:, :], ACT.Exp).then_inc(gs, 1)
            act.wait_ge(gs, GATE_STEPS)
            any_open = act.value_load(flag[0:1, 0:1], min_val=0, max_val=1)
            with act.If(any_open > 0):
                with act.Fori(0, TILES) as t:
                    act.wait_ge(r_xt, t + 1)
                    act.activation(xnt, g_ps[:, 0:D].rearrange("p (c n) -> p c n", c=DCH), ACT.Copy).then_inc(r_xtc, 1)
                    act.wait_ge(r_h, t + 1)
                    for i in range(2):
                        a = act.activation(hr[:, 4 * i:4 * i + 4, :].rearrange("p e n -> p (e n)"), s_ps[:, i, :], ACT.Relu)
                    a.then_inc(r_relu, 1)

        @block.gpsimd
        def _(pool):
            def turned_x(t, par):
                if isinstance(t, int) and t % (2 * GB) == 0:
                    pool.wait_ge(xt_in[t // (2 * GB)], 32)
                if not isinstance(t, int) or t >= 2:
                    pool.wait_ge(s_ready, t - 1)
                src = xt_sb[:, :, par, bass.ds((t // 2) * P if isinstance(t, int) else block_col(t, par), P)]
                if isinstance(t, int) and t < 2:
                    pool.tensor_copy(xt_hi[:, par, :, :], src).then_inc(xthi_first, 1)
                    pool.wait_ge(xthi_first, t + 1)
                else:
                    pool.tensor_copy(xt_hi[:, par, :, :], src).then_inc(xthi_done, 1)
                    wait_apart(pool, xthi_done, t - 1)
                pool.tensor_tensor(xt_lo[:, par, :, :], src, xt_hi[:, par, :, :].bitcast(F32), ALU.subtract).then_inc(xt_ready, 1)

            def block_col(t, par):
                return (t - par) * (P // 2)

            def rstd_x(i):
                pool.wait_ge(var1_done, i + 1)
                at = slice(*STATS[i])
                pool.tensor_tensor(rstd1[:, at], var1[:, at], pow_neg[:, 0:at.stop - at.start], ALU.pow).then_inc(rstd1_done, 1)

            def normalise(t, par, half):
                pool.wait_ge(recip_ready, 2 * t + half + 1)
                rows = probs[:, par, half * HALF:(half + 1) * HALF].rearrange("p (h k) -> p h k", k=TK)
                hs = slice(half * H // 2, (half + 1) * H // 2)
                pool.tensor_tensor(rows, rows, recip[:, par, hs].unsqueeze(2).broadcast_to([P, H // 2, TK]),
                                   ALU.mult).then_inc(probs_ready, 1)

            def step(t, par):
                normalise(t, par, 0)
                if isinstance(t, int) and t == 0:
                    normalise(t, par, 1)
                    turned_x(t + 2, par)
                else:
                    if live(t + 2, TILES):
                        turned_x(t + 2, par)
                    normalise(t, par, 1)
                pool.tensor_tensor(xb_sb[:, par, :], x_sb[:, t, :], bo_sb[:, :], ALU.add).then_inc(xb_ready, 1)

            pool.memset(ident[:, :], 0.0).then_inc(const_ready, 1)
            pool.memset(pow_neg[:, :], -0.5).then_inc(const_ready, 1)
            pool.memset(pow_pos[:, :], 0.5).then_inc(const_ready, 1)
            pool.wait_ge(const_ready, 3)
            pool.affine_select(out=ident[:, :], in_=ident[:, :], compare_op=ALU.not_equal, fill=1.0, base=0,
                               pattern=[[-1, P]], channel_multiplier=1).then_inc(const_ready, 1)
            turned_x(0, 0)
            turned_x(1, 1)
            for q in range(H // 2):
                hs = slice(2 * q, 2 * q + 2)
                pool.wait_ge(wohi_ready, q + 1)
                pool.tensor_tensor(wo_lo[:, hs, :], wo_sb[:, hs, :], wo_hi[:, hs, :].bitcast(F32), ALU.subtract).then_inc(wolo_ready, 1)
                if q == 2:
                    rstd_x(0)
            pool.wait_ge(ws2hi_ready, 1)
            pool.tensor_tensor(ws2_lo[:, :], ws2_sb[:, :], ws2_hi[:, :].bitcast(F32), ALU.subtract).then_inc(ws2lo_ready, 1)
            rstd_x(1)
            pool.wait_ge(bo_in, 16)
            pool.wait_ge(x_in[0], 32)
            step(0, 0)
            for i in range(1, 4):
                pool.wait_ge(xt_in[i], 32)
                pool.wait_ge(x_in[i], 32)
            step(1, 1)
            pairs(pool, 2, TG, step)
            rstd_x(2)
            pairs(pool, TG, TG + 2, step)
            rstd_x(3)
            pairs(pool, TG + 2, TILES - 2, step)
            for t in range(TILES - 2, TILES):
                step(t, t % 2)
            for tiles, done in ((slice(0, LAST), LAST), (slice(LAST, TILES), TILES)):
                pool.wait_ge(rvar2_done, done)
                pool.tensor_tensor(rstd2[:, tiles], rvar2[:, tiles], pow_pos[:, tiles], ALU.pow).then_inc(gs, 1)

        @block.vector
        def _(dve):
            def stats_of(t):
                dve.bn_stats(bn1[:, t, :], x_sb[:, t, :]).then_inc(bn1_done, 1)

            def aggregate_x(t):
                dve.wait_ge(bn1_done, t + 1)
                dve.bn_aggr(mv1[:, t, :], bn1[:, t, :]).then_inc(mv1_done, 1)

            def stats_x(i):
                for t in range(*STATS[i]):
                    if t % TG == 0:
                        dve.wait_ge(x_in[t // TG], 32)
                    stats_of(t)

            def variance_x(i):
                first, last = STATS[i]
                for t in range(last - 1 if i == 3 else first, last):
                    aggregate_x(t)
                dve.wait_ge(mv1_done, last)
                dve.tensor_scalar(var1[:, first:last], mv1[:, first:last, 1], EPS, None, ALU.add).then_inc(var1_done, 1)

            def stats_x1(t, par):
                dve.wait_ge(x1_ready, t + 1)
                dve.bn_stats(bn2[:, par, :], x1_tr[:, par, :]).then_inc(bn2_done, 1)

            def aggregate_x1(t, par):
                wait_apart(dve, bn2_done, t + 1)
                dve.bn_aggr(mv2[:, par, :], bn2[:, par, :]).then_inc(mv2_done, 1)

            def variance_x1(t, par):
                dve.wait_ge(mv2_done, t + 1)
                dve.tensor_scalar(var2[:, par:par + 1], mv2[:, par, 1:2], EPS, None, ALU.add).then_inc(var2_done, 1)

            def rvar_x1(t, par):
                dve.wait_ge(var2_done, t + 1)
                dve.reciprocal(rvar2[:, bass.ds(t, 1)], var2[:, par:par + 1]).then_inc(rvar2_done, 1)

            def maxima(t, par):
                dve.wait_ge(s_ready, t + 1)
                dve.tensor_reduce(row_max[:, par, :].rearrange("p (i h) -> p i h", i=2),
                                  s_ps[:, 2 * par:2 * par + 2, 0:HALF].rearrange("p i (h k) -> p i h k", k=TK),
                                  X, ALU.max).then_inc(max_done, 1)

            def neg_maxima(t, par):
                if isinstance(t, int) and t == 0:
                    dve.wait_ge(rstd1_done, 1)
                dve.wait_ge(max_done, t + 1)
                dve.tensor_scalar(neg_max[:, par, :], row_max[:, par, :], rstd1[:, bass.ds(t, 1)], -1.0,
                                  ALU.mult, ALU.mult).then_inc(negmax_ready, 1)

            def reciprocals(t, par, half):
                dve.wait_ge(exp_done, 2 * t + half + 1)
                hs = slice(half * H // 2, (half + 1) * H // 2)
                dve.reciprocal(recip[:, par, hs], sums[:, par, hs]).then_inc(recip_ready, 1)

            def lo_of_transposes(t, par):
                if late(t):
                    for pair in range(2):
                        at = slice(2 * pair * P, 2 * (pair + 1) * P)
                        dve.wait_ge(pthi_ready, pt_count(t, pair))
                        dve.tensor_tensor(pt_lo[:, at], (g_ps[:, 0:2 * P], s_ps[:, 2 * par, 0:2 * P])[pair], pt_hi[:, at].bitcast(F32),
                                          ALU.subtract).then_inc(ptlo_ready, 1)
                    return
                dve.wait_ge(pthi_ready, t + 1)
                dve.tensor_tensor(pt_lo[:, 0:PB], g_ps[:, 0:PB], pt_hi[:, 0:PB].bitcast(F32),
                                  ALU.subtract).then_inc(ptlo_ready, 1)

            def lo_of_last(t, par):
                dve.wait_ge(pthi_last, t + 1)
                n = last_columns(t)
                dve.tensor_tensor(pt_lo[:, PB:PB + n], g_ps[:, LO:LO + n], pt_hi[:, PB:PB + n].bitcast(F32),
                                  ALU.subtract).then_inc(ptlo_last, 1)

            def attended(t, par):
                dve.wait_ge(o_ready, t + 1)
                dve.wait_ge(xb_ready, t + 1)
                if not isinstance(t, int) or t >= 2:
                    dve.wait_ge(x1_kept, 8 * (t - par))
                dve.tensor_tensor(x1_tr[:, par, :], o_ps[:, 0:D], xb_sb[:, par, :], ALU.add).then_inc(x1_ready, 1)

            def squares(t, par):
                dve.wait_ge(relu_done, t + 1)
                dve.tensor_tensor(h2[:, par, :], h_relu[:, par, :], h_relu[:, par, :], ALU.mult).then_inc(h2_ready, 1)

            def top_logits(t, par):
                if late(t):
                    dve.wait_ge(last_logits, t - LAST + 1)
                    rows = s_ps[:, 2 * par + 1, 0:E]
                else:
                    wait_apart(dve, f_ready, t + 1)
                    rows = f_ps[:, D + FE:D + NL]
                dve.max(top8[:, par, :], rows).then_inc(top_done, 1)
                dve.tensor_copy(logits[:, t, :], rows).then_inc(logits_done, 1)
                dve.wait_ge(top_done, t + 1)
                dve.tensor_tensor(gap[:, bass.ds(t, 1)], top8[:, par, 1:2], top8[:, par, 0:1], ALU.subtract).then_inc(gap_done, 1)

            def result(t, par):
                if late(t):
                    dve.wait_ge(last_ready, t - LAST + 1)
                    rows = s_ps[:, 2 * par, 0:D]
                    x1_rows = x1_tr[:, par, :]
                else:
                    dve.wait_ge(f_ready, t + 2)
                    rows = f_ps[:, 0:D]
                    dve.wait_ge(x1_kept, 8 * (t - par) + 16)
                    x1_rows = x1_sb[:, t, :]
                dve.wait_ge(rvar2_done, t + 1)
                dve.scalar_tensor_tensor(out=y_sb[:, t, :], in0=rows, scalar=rvar2[:, bass.ds(t, 1)],
                                         in1=x1_rows, op0=ALU.mult, op1=ALU.add).then_inc(y_ready, 1)

            def step(t, par):
                lo_of_transposes(t, par)
                if live(t - 1, TILES):
                    stats_x1(t - 1, 1 - par)
                lo_of_last(t, par)
                if live(t - 1, TILES):
                    aggregate_x1(t - 1, 1 - par)
                maxima(t + 2, par)
                reciprocals(t + 1, 1 - par, 1)
                if live(t - 1, TILES):
                    variance_x1(t - 1, 1 - par)
                neg_maxima(t + 2, par)
                if live(t - 1, TILES):
                    rvar_x1(t - 1, 1 - par)
                    squares(t - 1, 1 - par)
                    top_logits(t - 1, 1 - par)
                attended(t, par)
                if live(t - 2, TILES):
                    result(t - 2, par)
                reciprocals(t + 2, par, 0)

            def lo_of_u(b, i, bank):
                dve.wait_ge(uhi_ready[b], i + 1)
                at = (slice(None), b, slice(2 * i, 2 * i + 2), slice(None))
                dve.tensor_tensor(u_lo[at], bank[:, :].rearrange("p (c d) -> p c d", c=2), u_hi[at].bitcast(F32),
                                  ALU.subtract).then_inc(ulo_ready[b], 1)

            dve.memset(mean_of[:, :], 1.0 / D).then_inc(fill_ready, 1)
            dve.memset(vt_hi[:, :, :].bitcast(F32), 0.0).then_inc(fill_ready, 1)
            dve.memset(vt_lo[:, :, :].bitcast(F32), 0.0).then_inc(fill_ready, 1)
            dve.memset(probs[:, :, HK:KC * P], 0.0).then_inc(fill_ready, 1)
            for i in range(2):
                hs = slice(i * H // 2, (i + 1) * H // 2)
                dve.wait_ge(wq_in[i], 16)
                dve.tensor_reduce(wq_mean[:, 0, hs], wqt_sb[:, hs, :], X, ALU.add).then_inc(wqs, 1)
                dve.wait_ge(wqs, 2 * i + 1)
                dve.tensor_scalar(wq_mean[:, 1, hs], wq_mean[:, 0, hs], 1.0 / D, None, ALU.mult).then_inc(wqs, 1)
                dve.wait_ge(wqs, 2 * i + 2)
                dve.tensor_tensor(wqt_sb[:, hs, :], wqt_sb[:, hs, :],
                                  wq_mean[:, 1, hs].unsqueeze(2).broadcast_to([P, H // 2, D]), ALU.subtract).then_inc(wq_ready, 1)
            for g in range(H // 2):
                dve.wait_ge(vthi_ready, g + 1)
                for h in (2 * g, 2 * g + 1):
                    v = dve.tensor_tensor(vt_heads(vt_lo)[:, h, :, P:P + TK],
                                          once_banks[g][:, (h % 2) * BK:(h % 2 + 1) * BK].rearrange("p (b n) -> p b n", b=B),
                                          vt_heads(vt_hi)[:, h, :, P:P + TK].bitcast(F32), ALU.subtract)
                v.then_inc(vtlo_ready, 1)
            for h in range(H):
                dve.wait_ge(ahi_ready, h + 1)
                at = (slice(None), slice(None), slice(None), slice(h * TK, (h + 1) * TK))
                dve.tensor_tensor(a_lo[at], a_banks[h][:, 0:DCH * BK].rearrange("p (c b k) -> p c b k", c=DCH, b=B),
                                  a_hi[at].bitcast(F32), ALU.subtract).then_inc(alo_ready, 1)
            dve.wait_ge(wmean_ready, 1)
            dve.tensor_tensor(wsr_c[:, :, :], wsr_sb[:, :, :],
                              s_ps[:, 2, 0:NL].unsqueeze(1).broadcast_to([P, DCH, NL]), ALU.subtract).then_inc(wsr_ready, 1)
            stats_x(0)
            variance_x(0)
            maxima(0, 0)
            neg_maxima(0, 0)
            maxima(1, 1)
            neg_maxima(1, 1)
            stats_x(1)
            variance_x(1)
            reciprocals(0, 0, 0)
            reciprocals(0, 0, 1)
            lo_of_u(0, 0, g_ps[:, 0:512])
            lo_of_u(0, 1, g_ps[:, 512:1024])
            stats_x(2)
            variance_x(2)
            reciprocals(1, 1, 0)
            lo_of_u(1, 0, g_ps[:, 0:512])
            dve.wait_ge(ulasthi_ready, 1)
            dve.tensor_tensor(u_lo[0:KLAST, :, KC - 1, :], f_ps[0:KLAST, :].rearrange("p (b d) -> p b d", b=B),
                              u_hi[0:KLAST, :, KC - 1, :].bitcast(F32), ALU.subtract).then_inc(ulastlo_ready, 1)
            lo_of_u(1, 1, o_ps)
            dve.wait_ge(rstd1_done, 2)
            for t in range(TG):
                step(t, t % 2)
                if t == 0:
                    dve.wait_ge(x_in[3], 32)
                stats_of(3 * TG + t)
                if t > 0:
                    aggregate_x(3 * TG + t - 1)
            variance_x(3)
            dve.wait_ge(rstd1_done, 3)
            pairs(dve, TG, 2 * TG, step)
            dve.wait_ge(rstd1_done, 4)
            pairs(dve, 2 * TG, TILES - 4, step)
            for t in range(TILES - 4, LAST):
                step(t, t % 2)
            for t in (LAST, LAST + 1):
                par = t % 2
                lo_of_transposes(t, par)
                if t > LAST:
                    top_logits(t - 2, par)
                    result(t - 3, 1 - par)
                lo_of_last(t, par)
                if t > LAST:
                    attended(t, par)
                stats_x1(t - 1, 1 - par)
                if t == LAST:
                    aggregate_x1(t - 1, 1 - par)
                    variance_x1(t - 1, 1 - par)
                    rvar_x1(t - 1, 1 - par)
                    reciprocals(t + 1, 1 - par, 1)
                    attended(t, par)
                    squares(t - 1, 1 - par)
            squares(LAST, 0)
            stats_x1(LAST + 1, 1)
            for part in (aggregate_x1, variance_x1, rvar_x1):
                for t in (LAST, LAST + 1):
                    part(t, t % 2)
            squares(LAST + 1, 1)
            result(LAST - 1, 1)
            for part in (result, top_logits):
                for t in (LAST, LAST + 1):
                    part(t, t % 2)

            dve.wait_ge(gs, 2)
            dve.wait_ge(gap_done, TILES)
            dve.tensor_tensor(gap_s[:, :], gap[:, :], rstd2[:, :], ALU.mult).then_inc(gs, 1)
            dve.wait_ge(gs, 4)
            dve.tensor_scalar(gap_d[:, :], gap_e[:, :], 1.0, None, ALU.add).then_inc(gs, 1)
            dve.wait_ge(gs, 5)
            dve.tensor_scalar(gate[:, :], gap_d[:, :], 1.0, None, ALU.is_le).then_inc(gs, 1)
            dve.wait_ge(gs, 6)
            dve.tensor_reduce(gate_any[:, :], gate[:, :], X, ALU.max).then_inc(gs, 1)
            dve.wait_ge(gs, 8)
            dve.tensor_scalar(flag[:, :], o_ps[0:1, 0:1], 0.0, None, ALU.is_gt).then_inc(gs, 1)
            dve.wait_ge(gs, GATE_STEPS)
            any_open = dve.value_load(flag[0:1, 0:1], min_val=0, max_val=1)
            with dve.If(any_open > 0):
                dve.wait_ge(x1_kept, 16 * NB)
                with dve.Fori(0, TILES) as t:
                    dve.bn_stats(r_bn[:, :], x1_sb[:, t, :]).then_inc(r_dve, 1)
                    dve.tensor_reduce(gate_max[:, :], logits[:, t, :], X, ALU.max).then_inc(r_dve, 1)
                    dve.wait_ge(r_dve, 11 * t + 2)
                    dve.tensor_scalar(gate_e[:, :], logits[:, t, :], gate_max[:, 0:1], gate[:, bass.ds(t, 1)],
                                      ALU.is_equal, ALU.mult).then_inc(r_dve, 1)
                    dve.bn_aggr(r_mv[:, :], r_bn[:, :]).then_inc(r_dve, 1)
                    dve.wait_ge(r_dve, 11 * t + 4)
                    dve.tensor_scalar(xn, x1_sb[:, t, :], r_mv[:, 0:1], rstd2[:, bass.ds(t, 1)],
                                      ALU.subtract, ALU.mult).then_inc(r_x, 1)
                    dve.wait_ge(r_relu, t + 1)
                    dve.tensor_tensor(hr[:, :, :], hr[:, :, :], hr[:, :, :], ALU.mult).then_inc(r_hc, 1)
                    dve.wait_ge(r_y, t + 1)
                    for e in range(E):
                        acc = dve.scalar_tensor_tensor(
                            out=y_sb[:, t, :], in0=routed_banks[e // 2][:, (e % 2) * D:(e % 2 + 1) * D],
                            scalar=gate_e[:, e:e + 1], in1=y_sb[:, t, :], op0=ALU.mult, op1=ALU.add)
                        if e < E - 1:
                            acc.then_inc(r_dve, 1)
                            dve.wait_ge(r_dve, 11 * t + 5 + e)
                    acc.then_inc(r_acc, 1)

    return nc


def kernel(x, ctx_768, L0_xattn_Wq, L0_xattn_Wk, L0_xattn_Wv, L0_xattn_Wo, L0_xattn_bo,
           L0_ffn_Ws1, L0_ffn_Ws2, L0_ffn_W1, L0_ffn_W2, L0_ffn_Wr):
    import numpy as np
    from concourse import bacc
    from concourse.bass_utils import run_bass_kernel_spmd

    x = np.asarray(x)
    context = np.asarray(ctx_768)
    arrays = {
        "x": x,
        "x_t": x.reshape(-1, x.shape[-1]).T,
        "ctx_t": context.reshape(-1, context.shape[-1]).T,
        "wq_t": np.asarray(L0_xattn_Wq).T,
        "wk": L0_xattn_Wk, "wv": L0_xattn_Wv, "wo": L0_xattn_Wo, "bo": L0_xattn_bo,
        "ws1": L0_ffn_Ws1, "ws2": L0_ffn_Ws2, "w1": L0_ffn_W1, "w2": L0_ffn_W2, "wr": L0_ffn_Wr,
    }
    arrays = {f"in_{name}": np.ascontiguousarray(a) for name, a in arrays.items()}
    nc = bacc.Bacc("TRN2", target_bir_lowering=False, num_devices=1)
    ins = [nc.dram_tensor(name, a.shape, mybir.dt.from_np(a.dtype), kind="ExternalInput").ap() for name, a in arrays.items()]
    out = nc.dram_tensor("out", x.shape, mybir.dt.from_np(x.dtype), kind="ExternalOutput").ap()
    program(nc, *ins, out)
    result = run_bass_kernel_spmd(nc, [arrays], core_ids=[0])
    return result.results[0]["out"]
```
